# Optimizing a Trainium2 kernel written in Bass

```python
import numpy as np
import jax
import jax.numpy as jnp

def _softmax(x, axis=-1):
    return jax.nn.softmax(x, axis=axis)

def _gelu(x):
    return jax.nn.gelu(x, approximate=True)

def _silu(x):
    return jax.nn.silu(x)

def _sigmoid(x):
    return jax.nn.sigmoid(x)

def _layernorm(x, axis=-1, eps=1e-05):
    m = jnp.mean(x, axis=axis, keepdims=True)
    v = jnp.var(x, axis=axis, keepdims=True)
    return (x - m) / jnp.sqrt(v + eps)

def _scatter_add(tgt, idx, src, axis=0):
    return tgt.at[idx].add(src)

def _segment_sum(src, seg, n):
    return jax.ops.segment_sum(src, seg, n)
kernel_name = 'mk_adj_ffn_d1_adj_r2_d765d9'

def setup_inputs(seed: int=0):
    np.random.seed(seed)
    _w = jnp.asarray

    def _rec_inputs():
        import jax
        import jax.numpy as jnp
        _gk = jax.random.key(seed)
        x = -0.0002928 + 1 * jax.random.normal(jax.random.fold_in(_gk, 1), (4096, 256), jnp.float32)
        _w = (1.0 + jnp.arange(4096, dtype=jnp.float32)) ** (-0.5)
        _w = _w / _w.mean()
        _pij = jnp.clip(0.00195312 * _w[:, None] * _w[None, :], 0.0, 1.0)
        _a = jax.random.uniform(jax.random.fold_in(_gk, 2), (4096, 4096)) < _pij
        _a = jnp.logical_or(_a, jnp.swapaxes(_a, -1, -2))
        _af = _a.astype(jnp.float32)
        adj = _af
        return (x, adj)
    x, adj = _rec_inputs()

    def _L0_gnn_setup():
        import jax, jax.numpy as jnp
        import numpy as np
        AVG_DEG = 32
        key = jax.random.key(seed)
        k1, k2, k3 = jax.random.split(key, 3)
        N, D_IN, D_OUT = (4096, 256, 256)
        x = jax.random.normal(k1, (N, D_IN), dtype=jnp.float32)
        u = jax.random.uniform(k2, (N, N), dtype=jnp.float32)
        A = (u < AVG_DEG / (2.0 * N)).astype(jnp.float32)
        A = A + A.T
        A = jnp.clip(A, 0.0, 1.0) * (1.0 - jnp.eye(N, dtype=jnp.float32))
        W = jax.random.normal(k3, (D_OUT, D_IN), dtype=jnp.float32) * (1.0 / np.sqrt(D_IN))
        b = jnp.zeros((D_OUT,), dtype=jnp.float32)
        return {'x': x, 'A': A, 'W': W, 'b': b}
    _L0_gnn_all = _L0_gnn_setup()
    _L0_gnn_in = {k: v for k, v in _L0_gnn_all.items() if k in ('W', 'b')}
    del _L0_gnn_all

    def _L0_ffn_setup():
        import jax, jax.numpy as jnp
        import numpy as np
        B, S, H, E, K = (8, 2048, 256, 8, 2)
        key = jax.random.key(seed)
        ks = jax.random.split(key, 7)
        s_h = 1.0 / np.sqrt(H)
        s_2h = 1.0 / np.sqrt(2 * H)
        return {'x': jax.random.normal(ks[0], (B, S, H), dtype=jnp.float32), 'gate_w': jax.random.uniform(ks[1], (H, E), minval=-s_h, maxval=s_h, dtype=jnp.float32), 'gate_b': jax.random.uniform(ks[2], (E,), minval=-s_h, maxval=s_h, dtype=jnp.float32), 'w1': jax.random.uniform(ks[3], (E, H, 2 * H), minval=-s_h, maxval=s_h, dtype=jnp.float32), 'b1': jax.random.uniform(ks[4], (E, 2 * H), minval=-s_h, maxval=s_h, dtype=jnp.float32), 'w2': jax.random.uniform(ks[5], (E, 2 * H, H), minval=-s_2h, maxval=s_2h, dtype=jnp.float32), 'b2': jax.random.uniform(ks[6], (E, H), minval=-s_2h, maxval=s_2h, dtype=jnp.float32)}
    _L0_ffn_all = _L0_ffn_setup()
    _L0_ffn_in = {k: v for k, v in _L0_ffn_all.items() if k in ('gate_w', 'gate_b', 'w1', 'b1', 'w2', 'b2')}
    del _L0_ffn_all
    return {'x': x, 'adj': adj, 'L0_gnn_W': _L0_gnn_in['W'], 'L0_gnn_b': _L0_gnn_in['b'], 'L0_ffn_gate_w': _L0_ffn_in['gate_w'], 'L0_ffn_gate_b': _L0_ffn_in['gate_b'], 'L0_ffn_w1': _L0_ffn_in['w1'], 'L0_ffn_b1': _L0_ffn_in['b1'], 'L0_ffn_w2': _L0_ffn_in['w2'], 'L0_ffn_b2': _L0_ffn_in['b2']}

def reference(x, adj, L0_gnn_W, L0_gnn_b, L0_ffn_gate_w, L0_ffn_gate_b, L0_ffn_w1, L0_ffn_b1, L0_ffn_w2, L0_ffn_b2):
    import jax
    import jax.numpy as jnp

    def _L0_gnn_ref(x, A, W, b):
        import jax, jax.numpy as jnp
        import numpy as np
        AVG_DEG = 32
        N = A.shape[0]
        A_t = A + jnp.eye(N, dtype=A.dtype)
        deg = jnp.sum(A_t, axis=1)
        d_inv_sqrt = jnp.where(deg > 0, jax.lax.rsqrt(deg), 0.0)
        adj_norm = A_t * d_inv_sqrt[:, None] * d_inv_sqrt[None, :]
        h = adj_norm @ x
        out = h @ W.T + b
        return jax.nn.relu(out)

    def _L0_ffn_ref(x, gate_w, gate_b, w1, b1, w2, b2):
        import jax, jax.numpy as jnp
        import numpy as np
        B, S, H, E, K = (8, 2048, 256, 8, 2)
        logits = jnp.einsum('bsh,he->bse', x, gate_w) + gate_b
        topk_vals, topk_idx = jax.lax.top_k(logits, K)
        topk_weights = jax.nn.softmax(topk_vals, axis=-1)
        mask = jax.nn.one_hot(topk_idx, E, dtype=topk_weights.dtype)
        weights = jnp.einsum('bske,bsk->bse', mask, topk_weights)
        h = jax.nn.relu(jnp.einsum('bsh,ehf->bsef', x, w1) + b1)
        expert_out = jnp.einsum('bsef,efh->bseh', h, w2) + b2
        return jnp.einsum('bseh,bse->bsh', expert_out, weights)
    x = x + _L0_gnn_ref(_layernorm(x, axis=-1), adj, L0_gnn_W, L0_gnn_b)
    x = x + _L0_ffn_ref(_layernorm(x, axis=-1)[None], L0_ffn_gate_w, L0_ffn_gate_b, L0_ffn_w1, L0_ffn_b1, L0_ffn_w2, L0_ffn_b2)[0]
    return x

_drawn_inputs = setup_inputs


def setup_inputs(seed=0):
    import zlib

    import numpy as np

    out = dict(_drawn_inputs(seed))
    spreads = {'L0_gnn_b': (0.0, 0.1)}
    factors = {'L0_ffn_b1': 5.489, 'L0_ffn_b2': 3.118}
    for name, (base, spread) in spreads.items():
        noise = np.random.default_rng([zlib.crc32(name.encode()), seed]).standard_normal(out[name].shape)
        drawn = base * np.exp(spread * noise) if base else spread * noise
        out[name] = jnp.asarray(drawn.astype(out[name].dtype))
    for name, factor in factors.items():
        out[name] = (out[name] * factor).astype(out[name].dtype)
    return out
```

```python
from contextlib import ExitStack

import concourse.bass as bass
from concourse import mybir

N, D = 4096, 256
E, F = 8, 512
P = 128
SB = 512
NSB = N // SB
NT = N // P
TPS = SB // P
KD = D // P
KF = F // P
PIECE_TILES = 2
PIECES = NT // PIECE_TILES * NSB
PPS = PIECES // NSB
PIECE = PIECE_TILES * SB
STAGES = 7
PSUM_GROUPS = 3
XS_SCALE = 128.0
W_SCALE = 64.0
EPS = 1e-5
ORDER = [NSB - 1] + list(range(NSB - 1))
PARTS = 2
KPP = NSB // PARTS
TPP = NT // PARTS
TOP = 2
SLOT_TILES = TPP * TOP + E - 1
C_IOTA_E = P
C_IOTA_T = C_IOTA_E + E
C_BEFORE = C_IOTA_T + SLOT_TILES
NCONST = C_BEFORE + E * E
TURNS = (SLOT_TILES - 3) // 4
AHEAD = 2
UNROLL = 4
DEG_FLOOR = 2.0 ** -10


def adjacency_slots():
    kept = sorted(((b, c) for b in range(NSB - 2) for c in range(NSB)), key=lambda k: (max(k), k))
    slots = {k: n for n, k in enumerate(kept)}
    for b in (NSB - 2, NSB - 1):
        for c in range(NSB):
            slots[b, c] = (b - (NSB - 2)) * NSB + c
    return slots, len(kept)


def timeline():
    groups = []
    for b in range(NSB):
        groups += [(b, b, half, 0, b + 1) for half in range(KD)]
        groups += [(b, i, half, b, b + 1) for i in range(b) for half in range(KD)]
    arrive = [5.0 + 1.8 * (n + 1) for n in range(PIECES)]
    tensor, timed = [], [(arrive[n], 0, ("piece", n)) for n in range(PIECES)]
    timed += [(arrive[PPS * b + 6], 0, ("norm", b)) for b in range(NSB)]
    now, piece = 0.0, 0
    scaled = [0.0] * NSB
    for b in range(NSB):
        for g, (step, i, half, c0, c1) in enumerate(groups):
            if step != b:
                continue
            while piece < PIECES and (piece < PPS * (b + 1) or arrive[piece] <= now):
                now = max(now, arrive[piece]) + 0.3
                tensor.append(("piece", piece))
                piece += 1
                if piece % PPS == 0:
                    timed.append((now, 1, ("prep", piece // PPS - 1)))
                    scaled[piece // PPS - 1] = now + 4.5
            tensor.append(("group", g))
            now = max(now, scaled[b]) + 1.75 * (c1 - c0)
            timed.append((now, 2, ("group", g)))
    last = [g for g, k in enumerate(groups) if k[0] == NSB - 1]
    tensor = [event for event in tensor if event not in [("group", g) for g in last]]
    timed = [event for _, _, event in sorted(timed) if event not in [("group", g) for g in last]]
    return groups, tensor, timed


def ending():
    order = []
    for k in range(NSB + 3):
        if k < NSB:
            order.append(("groups", k))
        for kind, lag in (("z", 1), ("t", 2), ("g", 3)):
            if 0 <= k - lag < NSB:
                order.append((kind, k - lag))
        if k >= 3 and (k - 2) % KPP == 0:
            order.append(("route", (k - 2) // KPP - 1))
    return order


def build(nc, x, adj_pieces, gnn_wT, gnn_b, gate_w, gate_b, w1, b1, w2, b2, consts, out):
    f32, f16, f8, bf16 = mybir.dt.float32, mybir.dt.float16, mybir.dt.float8e4, mybir.dt.bfloat16
    i32, u32 = mybir.dt.int32, mybir.dt.uint32
    ALU = mybir.AluOpType
    ACT = mybir.ActivationFunctionType
    AXX = mybir.AxisListType.X
    groups, tensor_order, vector_order = timeline()
    slots, nslots = adjacency_slots()
    ng = len(groups)
    last_groups = {k: [g for g, (b, i, *_) in enumerate(groups) if b == NSB - 1 and i == ORDER[k]]
                   for k in range(NSB)}

    ctx = ExitStack()
    with ctx:
        def sb(name, shape, dt):
            return ctx.enter_context(nc.sbuf_tensor(name, shape, dt))

        def sem(name):
            return ctx.enter_context(nc.semaphore(name))

        feats = sb("feats", [P, NSB, TPS * D], f32)
        xs = sb("xs", [P, NT, 2, D], f16)
        pool_words = sb("pool_words", [P, nslots * SB], f32)
        a8 = pool_words[:, :].bitcast(f8).rearrange("p (s n) -> p s n", s=nslots)
        stage = sb("stage", [P, STAGES, PIECE], f32)
        scratch = sb("scratch", [P, 256], f32)
        unequal = sb("unequal", [P, 2, PIECE], mybir.dt.bfloat16)
        mism = sb("mism", [P, PIECES], f32)
        ident = sb("ident", [P, P], f32)
        ones8 = sb("ones8", [P, 1], f8)
        stats = sb("stats", [P, TPS, 6], f32)
        stats_z = sb("stats_z", [P, TPS, 6], f32)
        mv_z = sb("mv_z", [P, TPS, 2], f32)
        newton_z = sb("newton_z", [P, 4, NT], f32)
        mv = sb("mv", [P, NT, 2], f32)
        newton = sb("newton", [P, 4, TPS], f32)
        minus_half = sb("minus_half", [P, NT], f32)
        var = sb("var", [P, NT], f32)
        deg = sb("deg", [P, NT], f32)
        rscale = sb("rscale", [P, NT], f32)

        dis_down = sb("dis_down", [P, NT], f32)
        wT = sb("wT", [P, KD, D], f32)
        bias_rows = sb("bias_rows", [P, D], f32)
        gate = sb("gate", [P, KD, E], f32)
        gate_bias = sb("gate_bias", [P, E], f32)
        b1_cols = sb("b1_cols", [P, E, KF], f32)
        zeros = sb("zeros", [P, D], f32)
        con = sb("con", [P, NCONST], f32)
        earlier = sb("earlier", [P, P], bf16)
        all_ones = sb("all_ones", [P, P], bf16)
        logits = sb("logits", [P, TPP, E], f32)
        top8 = sb("top8", [P, TPP, E], f32)
        idx8 = sb("idx8", [P, TPP, E], u32)
        idxf = sb("idxf", [P, TOP, TPP], f32)
        mask = sb("mask", [P, TOP, TPP, E], f32)
        mask_sum = sb("mask_sum", [P, TPP, E], bf16)
        rank = sb("rank", [P, TPP, E], f32)
        picked = sb("picked", [P, TPP, E], f32)
        counts_i = sb("counts_i", [P, 2, E], i32)
        tiles_f = sb("tiles_f", [P, E], f32)
        prod8 = sb("prod8", [P, E, E], f32)
        base = sb("base", [P, E], f32)
        ends = sb("ends", [P, E], f32)
        over = scratch[:, :].bitcast(bf16)[:, 0:SLOT_TILES * E].rearrange("p (t e) -> p t e", e=E)
        owner = sb("owner", [P, SLOT_TILES], f32)
        slot_f = sb("slot_f", [P, TOP, TPP], f32)
        top_gap = sb("top_gap", [P, TPP], f32)
        exp_gap = sb("exp_gap", [P, TPP], f32)
        denom = sb("denom", [P, TPP], f32)
        slot_of = sb("slot_of", [P, PARTS, TOP, TPP], u32)
        pair_w = sb("pair_w", [P, PARTS, TOP, TPP], f32)
        tile_e = sb("tile_e", [P, PARTS, -(-SLOT_TILES // 4) * 4], i32)

        def words(first_slot, slots_):
            return pool_words[:, first_slot * SB:(first_slot + slots_) * SB]

        w2s = words(0, 16).bitcast(f16).rearrange("p (e s k n) -> p e s k n", e=E, s=2, k=KF)
        w1s = words(16, 16).bitcast(f16).rearrange("p (e s k n) -> p e s k n", e=E, s=2, k=KD)
        gathered = [xs[:, :, :, :].rearrange("p t s d -> p (t s d)").bitcast(f32).rearrange("p (t r d) -> p t r d", t=TPP, r=TOP),
                    words(16, 16).rearrange("p (t r d) -> p t r d", t=TPP, r=TOP)]
        w2_in_sb = xs[:, :, :, :].rearrange("p t s d -> p (t s d)").bitcast(f32)
        normed_a = words(32, 8).rearrange("p (k t d) -> p k t d", k=KPP, d=D)
        x_again = [words(40, 2).rearrange("p (t d) -> p t d", d=D),
                   unequal[:, :, :].rearrange("p a n -> p (a n)").bitcast(f32).rearrange("p (t d) -> p t d", d=D)]
        b2_rows = words(42, 4).rearrange("p (e d) -> p e d", e=E)
        xT_parts = words(46, 1).bitcast(f16).rearrange("p (r s k n) -> p r s k n", r=2, s=2, k=KD)
        y_sb = words(47, 1).rearrange("p (r d) -> p r d", r=2)
        xT_gate = stage[:, 6, :].rearrange("p (k n) -> p k n", k=KD)
        w1_in_sb = stage[:, 4:6, :]
        h_sb = stage[:, 4, :].rearrange("p (r k n) -> p r k n", r=2, k=KF)
        h_parts = stage[:, 5, :].bitcast(f16).rearrange("p (r s k n) -> p r s k n", r=2, s=2, k=KF)
        sorted_in = stage[:, 6, :].rearrange("p (r d) -> p r d", r=4)

        def normed(k):
            return normed_a[:, k] if k < KPP else stage[:, k - KPP, :].rearrange("p (t d) -> p t d", d=D)

        x_sorted = [nc.dram_tensor(f"x_sorted{n}", (SLOT_TILES * P, D), f32).ap() for n in range(PARTS)]
        y_sorted = [nc.dram_tensor(f"y_sorted{n}", (SLOT_TILES * P, D), f32).ap() for n in range(PARTS)]

        degree = [ctx.enter_context(nc.psum_tensor(f"degree{n}", [P, 512], f32)) for n in range(2)]
        banks = [ctx.enter_context(nc.psum_tensor(f"bank{n}", [P, 512], f32)) for n in range(6)]

        x_in = sem("x_in")

        adj_in = [sem(f"adj_in{n}") for n in range(STAGES)]
        chain = sem("chain")
        ident_made = sem("ident_made")
        deg_read = sem("deg_read")
        pow_ready = sem("pow_ready")
        diag_added = sem("diag_added")
        piece_cast = sem("piece_cast")
        piece_checked = sem("piece_checked")
        piece_compared = sem("piece_compared")
        difference_summed = sem("difference_summed")
        deg_summed = sem("deg_summed")
        deg_safe = sem("deg_safe")
        xs_ready = sem("xs_ready")
        group_done = sem("group_done")
        first_stored = sem("first_stored")
        rest_added = sem("rest_added")
        weights_in = sem("weights_in")
        zeros_made = sem("zeros_made")
        rows_zeroed = sem("rows_zeroed")
        x_again_in = [sem(f"x_again_in{n}") for n in range(2)]
        w1_in = [sem(f"w1_in{n}") for n in range(2)]
        w1_high = sem("w1_high")
        w1_low = sem("w1_low")
        w2_in = sem("w2_in")
        w2_high = sem("w2_high")
        w2_low = sem("w2_low")
        b2_in = sem("b2_in")
        norm_safe = sem("norm_safe")
        norm_pow = sem("norm_pow")
        z_done = sem("z_done")
        z_used = sem("z_used")
        normed_ready = sem("normed_ready")
        turned = sem("turned")
        turned_out = sem("turned_out")
        gate_done = sem("gate_done")
        logits_read = sem("logits_read")
        masks_ready = sem("masks_ready")
        ranked = sem("ranked")
        rank_read = sem("rank_read")
        slots_ready = sem("slots_ready")
        gap_ready = sem("gap_ready")
        exp_ready = sem("exp_ready")
        pair_w_ready = sem("pair_w_ready")
        consts_cast = sem("consts_cast")
        scattered = [sem(f"scattered{n}") for n in range(PARTS)]
        sorted_load = [sem(f"sorted_load{n}") for n in range(4)]
        tile_turned = sem("tile_turned")
        xT_high = sem("xT_high")
        xT_low = sem("xT_low")
        h_summed = sem("h_summed")
        h_relu = sem("h_relu")
        h_high = sem("h_high")
        h_low = sem("h_low")
        y_summed = sem("y_summed")
        y_ready = sem("y_ready")
        y_stored = [sem(f"y_stored{n}") for n in range(2)]
        fetched = [sem(f"fetched{n}") for n in range(NSB)]
        summed_out = sem("summed_out")
        out_sent = sem("out_sent")

        block = ctx.enter_context(nc.Block())
        x_tiles = x.rearrange("(t p) d -> p t d", p=P)
        out_tiles = out.rearrange("(t p) d -> p t d", p=P)
        feats_rows = feats[:, :, :].rearrange("p b (t d) -> p (b t) d", d=D)
        feats_cols = feats[:, :, :].rearrange("p b (h i) -> p b h i", h=KD)

        firsts = [g for g in range(ng) if groups[g][0] == groups[g][1]]
        rests = [g for g in range(ng) if groups[g][0] != groups[g][1]]

        def wait_evacuated(eng, g):
            if g in firsts:
                eng.wait_ge(first_stored, firsts.index(g) + 1)
            else:
                eng.wait_ge(rest_added, rests.index(g) + 1)

        def on_pool(n):
            return n % 8 in (2, 5, 7)

        def wait_checked(eng, n):
            mine = sum(on_pool(m) == on_pool(n) for m in range(n + 1))
            eng.wait_ge(piece_compared if on_pool(n) else piece_checked, mine)

        def a8_piece(n):
            b, q = divmod(n, PPS)
            c, half = divmod(q, TPS // PIECE_TILES)
            return a8[:, slots[b, c], half * PIECE:(half + 1) * PIECE]

        def expert_of(eng, part, tile):
            return eng.value_load(tile_e[0:1, part, bass.ds(tile, 1)], min_val=0, max_val=E - 1)

        def experts_of(eng, part, tile, count):
            registers = [eng.alloc_register(f"expert_{part}_{n}") for n in range(count)]
            eng.load(registers, tile_e[0:1, part, bass.ds(tile, count)])
            return [eng.snap(r, min_val=0, max_val=E - 1) for r in registers]

        def adj_arrived(eng, n):
            eng.wait_ge(adj_in[n % STAGES], 16 * (n // STAGES + 1))

        def diag_pieces(n):
            return sum(m // PPS == m % PPS * PIECE_TILES // TPS for m in range(n))

        @block.sync
        def _(sp):
            for n in range(PIECES):
                if n >= STAGES:
                    wait_checked(sp, n - STAGES)
                    sp.wait_ge(piece_cast, n - STAGES + 1)
                sp.dma_start(stage[:, n % STAGES, :], adj_pieces[n]).then_inc(adj_in[n % STAGES], 16)
            sp.wait_ge(piece_cast, PIECES)
            wait_checked(sp, PIECES - 1)
            wait_checked(sp, PIECES - 2)
            for e in range(E):
                if e >= 2:
                    sp.wait_ge(w1_low, e - 1)
                sp.dma_start(w1_in_sb[:, e % 2, :].rearrange("p (k f) -> p k f", k=KD),
                             w1[e].rearrange("(k p) f -> p k f", p=P)).then_inc(w1_in[e % 2], 16)
            sp.wait_ge(group_done, ng)
            for e in range(E):
                sp.dma_start(w2_in_sb.rearrange("p (e k d) -> p e k d", e=E, k=KF)[:, e],
                             w2[e].rearrange("(k p) d -> p k d", p=P)).then_inc(w2_in, 16)
            sp.dma_start(b2_rows.rearrange("p e d -> p (e d)"), b2.partition_broadcast(P)).then_inc(b2_in, 16)

            sp.wait_ge(w1_low, E)
            sp.wait_ge(gate_done, NSB)
            for part in range(PARTS):
                sp.wait_ge(scattered[part], 16 * TOP * TPP)

                first = part * SLOT_TILES
                for tile in range(3):
                    if first + tile >= 4:
                        sp.wait_ge(tile_turned, first + tile - 3)
                    sp.dma_start(sorted_in[:, (first + tile) % 4, :],
                                 x_sorted[part][tile * P:(tile + 1) * P, :]).then_inc(sorted_load[(first + tile) % 4], 16)
                with sp.Fori(0, TURNS) as turn:
                    for u in range(UNROLL):
                        tile = turn * UNROLL + u
                        n = tile + first
                        sp.wait_ge(tile_turned, n + 1)
                        sp.dma_start(sorted_in[:, (first + u + 3) % 4, :],
                                     x_sorted[part][bass.ds((tile + 3) * P, P), :]).then_inc(sorted_load[(first + u + 3) % 4], 16)
            for k in range(NSB):
                sp.wait_ge(summed_out, k + 1)
                sp.dma_start(out_tiles[:, ORDER[k] * TPS:(ORDER[k] + 1) * TPS, :],
                             feats_rows[:, ORDER[k] * TPS:(ORDER[k] + 1) * TPS, :]).then_inc(out_sent, 16)
            sp.wait_ge(out_sent, 16 * NSB)

        @block.gpsimd
        def _(pool):
            nc.gpsimd.memset(zeros[:, :], 0.0).then_inc(zeros_made, 1)
            nc.gpsimd.memset(minus_half[:, :], -0.5).then_inc(ident_made, 1)
            nc.gpsimd.memset(ident[:, :], 0.0).then_inc(ident_made, 1)
            nc.gpsimd.memset(ones8[:, :], 1.0).then_inc(ident_made, 1)
            pool.wait_ge(ident_made, 3)
            nc.gpsimd.affine_select(out=ident[:, :], in_=ident[:, :], compare_op=ALU.not_equal, fill=1.0,
                                    base=0, pattern=[[-1, P]], channel_multiplier=1).then_inc(ident_made, 1)
            pool.wait_ge(ident_made, 4)
            for kind, n in vector_order:
                if kind == "piece" and diag_pieces(n + 1) > diag_pieces(n):
                    adj_arrived(pool, n)
                    first = n % PPS * PIECE_TILES % TPS * P
                    for t in range(PIECE_TILES):
                        part = stage[:, n % STAGES, t * SB + first + t * P:t * SB + first + (t + 1) * P]
                        last = nc.gpsimd.tensor_tensor(part, part, ident[:, :], ALU.add)
                    last.then_inc(diag_added, 1)
                if kind == "piece" and on_pool(n):
                    pool.wait_ge(piece_cast, n + 1)
                    done = sum(on_pool(m) for m in range(n))
                    if done >= 2:
                        pool.wait_ge(difference_summed, done - 1)
                    nc.gpsimd.tensor_tensor(unequal[:, done % 2, :], stage[:, n % STAGES, :], a8_piece(n),
                                            ALU.subtract).then_inc(piece_compared, 1)
                if kind == "prep":
                    pool.wait_ge(deg_safe, n + 1)
                    nc.gpsimd.tensor_tensor(newton[:, 3, 0:TPS], newton[:, 0, 0:TPS], minus_half[:, 0:TPS],
                                            ALU.pow).then_inc(pow_ready, 1)

            def power(n, width):
                pool.wait_ge(norm_safe, n + 1)
                nc.gpsimd.tensor_tensor(newton_z[:, 3, 0:width], newton_z[:, 0, 0:width], minus_half[:, 0:width],
                                        ALU.pow).then_inc(norm_pow, 1)

            def scatter(part, pairs):
                pool.wait_ge(rows_zeroed, 16 * PARTS)
                pool.wait_ge(slots_ready, part + 1)
                for r, t in (divmod(pair, TPP) for pair in pairs):
                    nc.gpsimd.indirect_dma_start(
                        out=x_sorted[part][:, :],
                        out_offset=bass.IndirectOffsetOnAxis(ap=slot_of[:, part, r, t:t + 1], axis=0),
                        in_=normed(part * KPP + t // TPS)[:, t % TPS, :], in_offset=None).then_inc(scattered[part], 16)

            power(0, NT)
            for k in range(KPP + 2):
                power(1 + k, TPS)
            scatter(0, range(0, 8))
            power(1 + KPP + 2, TPS)
            scatter(0, range(8, 16))
            power(1 + KPP + 3, TPS)
            scatter(0, range(16, TOP * TPP))
            scatter(1, range(TOP * TPP))
            for part in range(PARTS):
                last_tile = (part + 1) * SLOT_TILES
                for parity in range(2):
                    tiles = sum(n % 2 == parity for n in range(last_tile))
                    pool.wait_ge(y_stored[parity], 16 * (tiles + 1))
                if part == 0:
                    pool.wait_ge(w2_low, E)
                for t in range(TPP):
                    for r in range(TOP):
                        nc.gpsimd.indirect_dma_start(
                            out=gathered[part][:, t, r, :], out_offset=None, in_=y_sorted[part][:, :],
                            in_offset=bass.IndirectOffsetOnAxis(ap=slot_of[:, part, r, t:t + 1], axis=0),
                        ).then_inc(fetched[part * KPP + t // TPS], 16)

        @block.scalar
        def _(act):
            def sum_difference(n):
                done = sum(on_pool(k) for k in range(n))
                act.wait_ge(piece_compared, done + 1)
                part = unequal[:, done % 2, :]
                nc.scalar.activation(part, part, ACT.Abs, accum_out=mism[:, n:n + 1]).then_inc(difference_summed, 1)

            def load_x_again(k):
                act.dma_start(x_again[k % 2], x_tiles[:, ORDER[k] * TPS:(ORDER[k] + 1) * TPS, :]).then_inc(x_again_in[k % 2], 16)

            def store_first(g):
                _, i, half, _, _ = groups[g]
                act.wait_ge(group_done, g + 1)
                nc.scalar.activation(feats_cols[:, i, half, :], banks[g % PSUM_GROUPS][:, :],
                                     ACT.Copy).then_inc(first_stored, 1)

            act.dma_start(feats_rows, x_tiles).then_inc(x_in, 16)
            for target, source in ((wT[:, :, :], gnn_wT.rearrange("(k p) n -> p k n", p=P)),
                                   (bias_rows[:, :], gnn_b[0, :].partition_broadcast(P)),
                                   (gate[:, :, :], gate_w.rearrange("(k p) e -> p k e", p=P)),
                                   (gate_bias[:, :], gate_b[0, :].partition_broadcast(P)),
                                   (b1_cols[:, :, :], b1), (con[:, :], consts)):
                act.dma_start(target, source).then_inc(weights_in, 16)
            for kind, n in vector_order:
                if kind == "piece":
                    adj_arrived(act, n)
                    if diag_pieces(n + 1) > diag_pieces(n):
                        act.wait_ge(diag_added, diag_pieces(n + 1))
                    if n % PPS == 0 and n // PPS >= NSB - 2:
                        act.wait_ge(group_done, sum(k[0] <= n // PPS - 4 for k in groups))
                    nc.scalar.activation(a8_piece(n), stage[:, n % STAGES, :], ACT.Copy, saturate=False).then_inc(piece_cast, 1)
                    if n >= 4 and on_pool(n - 4):
                        sum_difference(n - 4)
                if kind == "group" and n in firsts:
                    store_first(n)
            for n in range(PIECES - 4, PIECES):
                if on_pool(n):
                    sum_difference(n)

            act.wait_ge(zeros_made, 1)
            for part in range(PARTS):
                act.dma_start(x_sorted[part].rearrange("(t p) d -> p t d", p=P),
                              zeros[:, :].unsqueeze(1).to_broadcast([P, SLOT_TILES, D])).then_inc(rows_zeroed, 16)
            for e in range(E):
                act.wait_ge(w1_in[e % 2], 16 * (e // 2 + 1))
                if e == 0:
                    act.wait_ge(group_done, sum(g[0] <= NSB - 3 for g in groups))
                nc.scalar.activation(w1s[:, e, 0], w1_in_sb[:, e % 2, :].rearrange("p (k n) -> p k n", k=KD),
                                     ACT.Copy, scale=W_SCALE).then_inc(w1_high, 1)
            act.wait_ge(group_done, sum(g[0] <= NSB - 2 for g in groups))
            act.wait_ge(difference_summed, sum(on_pool(n) for n in range(PIECES)))
            for k in range(2):
                load_x_again(k)
            for kind, k in ending():
                if kind == "groups":
                    for g in last_groups[k]:
                        if g in firsts:
                            store_first(g)
                elif kind == "z" and k + 2 < NSB:
                    act.wait_ge(z_used, k + 1)
                    load_x_again(k + 2)
                elif kind == "t":
                    act.wait_ge(turned, k + 1)
                    if k == 0:
                        wait_checked(act, PIECES - 2)
                    else:
                        act.wait_ge(gate_done, k)
                    for half in range(KD):
                        last = nc.scalar.activation(xT_gate[:, half, :], banks[4 + half][:, :], ACT.Copy)
                    last.then_inc(turned_out, 1)
                elif kind == "route":
                    act.wait_ge(gap_ready, k + 1)
                    nc.scalar.activation(exp_gap[:, :], top_gap[:, :], ACT.Exp).then_inc(exp_ready, 1)
            act.wait_ge(w2_in, 16 * E)
            for e in range(E):
                nc.scalar.activation(w2s[:, e, 0].rearrange("p k d -> p (k d)"), w2_in_sb[:, e * KF * D:(e + 1) * KF * D],
                                     ACT.Copy, scale=W_SCALE).then_inc(w2_high, 1)

            def xT_high_part(n, parity):
                act.wait_ge(tile_turned, n + 1)
                act.wait_ge(h_summed, n - 1 + AHEAD)
                nc.scalar.activation(xT_parts[:, parity, 0].rearrange("p k n -> p (k n)"), degree[parity][:, 0:D],
                                     ACT.Copy).then_inc(xT_high, 1)

            def relu(n, parity, e):
                act.wait_ge(h_summed, n + 1 + AHEAD)
                act.wait_ge(h_low, n - 1 + AHEAD)
                for f in range(KF):
                    last = nc.scalar.activation(
                        h_sb[:, parity, f, :], banks[parity][:, f * P:(f + 1) * P], ACT.Relu,
                        bias=b1_cols[:, bass.ds(e, 1), f:f + 1].rearrange("p a b -> p (a b)"), scale=1.0 / W_SCALE)
                last.then_inc(h_relu, 1)

            def store_rows(part, tile, n, parity):
                act.wait_ge(y_ready, n + 1 + AHEAD)
                act.dma_start(y_sorted[part][bass.ds(tile * P, P), :], y_sb[:, parity, :]).then_inc(y_stored[parity], 16)

            act.wait_ge(w2_low, E)
            for buffer_stored in y_stored:
                act.sem_inc(buffer_stored, 16)
            for part in range(PARTS):
                first = part * SLOT_TILES
                xT_high_part(first, first % 2)
                xT_high_part(first + 1, (first + 1) % 2)
                relu(first, first % 2, expert_of(act, part, 0))
                with act.Fori(0, TURNS) as turn:
                    es = experts_of(act, part, turn * UNROLL, UNROLL + 1)
                    for u in range(UNROLL):
                        n = turn * UNROLL + u + first
                        xT_high_part(n + 2, (first + u) % 2)
                        relu(n + 1, (first + u + 1) % 2, es[u + 1])
                        store_rows(part, turn * UNROLL + u, n, (first + u) % 2)
                for tile in range(TURNS * UNROLL, SLOT_TILES):
                    n = first + tile
                    if tile + 2 < SLOT_TILES:
                        xT_high_part(n + 2, n % 2)
                    if tile + 1 < SLOT_TILES:
                        relu(n + 1, (n + 1) % 2, expert_of(act, part, tile + 1))
                    store_rows(part, tile, n, n % 2)

        @block.vector
        def _(dve):
            links = [0]

            def link(ins):
                links[0] += 1
                ins.then_inc(chain, 1)
                dve.wait_ge(chain, links[0])

            def refine(v, y, t, u):
                link(nc.vector.tensor_tensor(t, y, y, ALU.mult))
                link(nc.vector.tensor_tensor(u, t, v, ALU.mult))
                link(nc.vector.tensor_scalar(t, u, -0.5, 1.5, ALU.mult, ALU.add))
                link(nc.vector.tensor_tensor(y, y, t, ALU.mult))

            def add_group(n):
                _, i, half, _, _ = groups[n]
                dve.wait_ge(group_done, n + 1)
                dve.wait_ge(first_stored, KD * (i + 1))
                if rests.index(n):
                    dve.wait_ge(rest_added, rests.index(n))
                nc.vector.tensor_tensor(feats_cols[:, i, half, :], feats_cols[:, i, half, :],
                                        banks[n % PSUM_GROUPS][:, :], ALU.add).then_inc(rest_added, 1)

            def linear_and_norm(k):
                i = ORDER[k]
                dve.wait_ge(z_done, k + 1)
                dve.wait_ge(x_again_in[k % 2], 16 * (k // 2 + 1))
                tiles = [feats_rows[:, i * TPS + j, :] for j in range(TPS)]
                for j in range(TPS):
                    last = nc.vector.scalar_tensor_tensor(
                        out=tiles[j], in0=degree[j // 2][:, j % 2 * D:(j % 2 + 1) * D],
                        scalar=dis_down[:, i * TPS + j:i * TPS + j + 1], in1=bias_rows[:, :], op0=ALU.mult, op1=ALU.add)
                link(last)
                for j in range(TPS):
                    last = nc.vector.scalar_tensor_tensor(out=tiles[j], in0=tiles[j], scalar=0.0, in1=x_again[k % 2][:, j, :],
                                                          op0=ALU.max, op1=ALU.add)
                last.then_inc(z_used, 1)
                dve.wait_ge(z_used, k + 1)
                for j in range(TPS):
                    last = nc.vector.bn_stats(stats_z[:, j, :], tiles[j])
                link(last)
                for j in range(TPS):
                    last = nc.vector.bn_aggr(mv_z[:, j, :], stats_z[:, j, :])
                link(last)
                v, t, u, y = (newton_z[:, n, 0:TPS] for n in range(4))
                nc.vector.tensor_scalar(v, mv_z[:, :, 1], EPS, None, ALU.add).then_inc(norm_safe, 1)
                dve.wait_ge(norm_safe, k + 2)
                dve.wait_ge(norm_pow, k + 2)
                refine(v, y, t, u)
                if k == 0:
                    dve.wait_ge(group_done, sum(g[0] <= NSB - 2 for g in groups))
                if k == KPP:
                    wait_checked(dve, PIECES - 1)
                for j in range(TPS):
                    last = nc.vector.tensor_scalar(normed(k)[:, j, :], tiles[j], mv_z[:, j, 0:1], newton_z[:, 3, j:j + 1],
                                                   ALU.subtract, ALU.mult)
                last.then_inc(normed_ready, 1)

            def top_two(k):
                dve.wait_ge(gate_done, k + 1)
                if k == KPP:
                    dve.wait_ge(pair_w_ready, 1)
                rows = slice(k % KPP * TPS, (k % KPP + 1) * TPS)
                nc.vector.tensor_tensor(logits[:, rows, :], banks[3][:, 0:TPS * E].rearrange("p (t e) -> p t e", e=E),
                                        gate_bias[:, :].unsqueeze(1).to_broadcast([P, TPS, E]),
                                        ALU.add).then_inc(logits_read, 1)
                dve.wait_ge(logits_read, k + 1)
                for t in range(rows.start, rows.stop):
                    last = nc.vector.max(top8[:, t, :], logits[:, t, :])
                link(last)
                for t in range(rows.start, rows.stop):
                    last = nc.vector.max_index(idx8[:, t, :], top8[:, t, :], logits[:, t, :])
                link(last)

            def route(part):
                nc.vector.tensor_tensor(top_gap[:, :], top8[:, :, 1], top8[:, :, 0], ALU.subtract).then_inc(gap_ready, 1)
                for r in range(TOP):
                    link(nc.vector.tensor_copy(idxf[:, r, :], idx8[:, :, r]))
                    link(nc.vector.tensor_tensor(mask[:, r], iota_e.unsqueeze(1).to_broadcast([P, TPP, E]),
                                                 idxf[:, r, :].unsqueeze(2).to_broadcast([P, TPP, E]), ALU.is_equal))
                nc.vector.tensor_tensor(mask_sum[:, :, :], mask[:, 0], mask[:, 1], ALU.add).then_inc(masks_ready, 1)
                dve.wait_ge(exp_ready, part + 1)
                link(nc.vector.tensor_scalar(denom[:, :], exp_gap[:, :], 1.0, None, ALU.add))
                link(nc.vector.reciprocal(pair_w[:, part, 0, :], denom[:, :]))
                nc.vector.tensor_tensor(pair_w[:, part, 1, :], exp_gap[:, :], pair_w[:, part, 0, :],
                                        ALU.mult).then_inc(pair_w_ready, 1)
                dve.wait_ge(ranked, part + 1)
                link(nc.vector.tensor_copy(rank[:, :, :], banks[3][:, 0:TPP * E].rearrange("p (t e) -> p t e", e=E)))
                nc.vector.tensor_scalar(counts_i[:, 0, :], banks[3][:, TPP * E:(TPP + 1) * E], float(P - 1), None,
                                        ALU.add).then_inc(rank_read, 1)
                dve.wait_ge(rank_read, part + 1)
                link(nc.vector.tensor_scalar(counts_i[:, 1, :], counts_i[:, 0, :], P.bit_length() - 1, None,
                                             ALU.logical_shift_right))
                link(nc.vector.tensor_copy(tiles_f[:, :], counts_i[:, 1, :]))
                link(nc.vector.tensor_tensor(prod8[:, :, :], before, tiles_f[:, :].unsqueeze(1).to_broadcast([P, E, E]),
                                             ALU.mult))
                link(nc.vector.tensor_reduce(base[:, :], prod8[:, :, :], AXX, ALU.add))
                link(nc.vector.scalar_tensor_tensor(out=ends[:, :], in0=base[:, :], scalar=1.0 / P, in1=tiles_f[:, :],
                                                    op0=ALU.mult, op1=ALU.add))
                link(nc.vector.tensor_tensor(rank[:, :, :], rank[:, :, :],
                                             base[:, :].unsqueeze(1).to_broadcast([P, TPP, E]), ALU.add))
                for r in range(TOP):
                    link(nc.vector.tensor_tensor(picked[:, :, :], mask[:, r], rank[:, :, :], ALU.mult))
                    link(nc.vector.tensor_reduce(slot_f[:, r, :], picked[:, :, :], AXX, ALU.add))
                link(nc.vector.tensor_tensor(over[:, :, :], iota_t.unsqueeze(2).to_broadcast([P, SLOT_TILES, E]),
                                             ends[:, :].unsqueeze(1).to_broadcast([P, SLOT_TILES, E]), ALU.is_ge))
                link(nc.vector.tensor_reduce(owner[:, :], over[:, :, :], AXX, ALU.add))
                link(nc.vector.tensor_scalar(tile_e[:, part, 0:SLOT_TILES], owner[:, :], float(E - 1), None, ALU.min))
                nc.vector.tensor_copy(slot_of[:, part], slot_f[:, :, :]).then_inc(slots_ready, 1)
                dve.wait_ge(slots_ready, part + 1)

            dve.wait_ge(x_in, 16)
            for kind, n in vector_order:
                if kind == "norm":
                    if n:
                        dve.wait_ge(xs_ready, n)
                    for k in range(TPS):
                        last = nc.vector.bn_stats(stats[:, k, :], feats_rows[:, n * TPS + k, :])
                    link(last)
                    for k in range(TPS):
                        last = nc.vector.bn_aggr(mv[:, n * TPS + k, :], stats[:, k, :])
                    link(last)
                    cols = slice(n * TPS, (n + 1) * TPS)
                    link(nc.vector.tensor_scalar(var[:, cols], mv[:, cols, 1], EPS, XS_SCALE ** -2, ALU.add, ALU.mult))
                elif kind == "piece":
                    if on_pool(n):
                        continue
                    dve.wait_ge(piece_cast, n + 1)
                    if n:
                        dve.wait_ge(piece_checked, sum(not on_pool(m) for m in range(n)))
                    nc.vector.scalar_tensor_tensor(
                        out=scratch[:, :].bitcast(mybir.dt.uint8), in0=stage[:, n % STAGES, :], scalar=1.0, in1=a8_piece(n),
                        op0=ALU.mult, op1=ALU.not_equal, accum_out=mism[:, n:n + 1]).then_inc(piece_checked, 1)
                elif kind == "prep":
                    dve.wait_ge(deg_summed, PPS * (n + 1))
                    cols = slice(n * TPS, (n + 1) * TPS)
                    v, y = newton[:, 0, :], newton[:, 3, :]
                    nc.vector.tensor_copy(deg[:, cols], degree[n % 2][:, 0:TPS]).then_inc(deg_read, 1)
                    dve.wait_ge(deg_read, n + 1)
                    nc.vector.scalar_tensor_tensor(out=v, in0=deg[:, cols], scalar=DEG_FLOOR, in1=var[:, cols],
                                                   op0=ALU.max, op1=ALU.mult).then_inc(deg_safe, 1)
                    dve.wait_ge(deg_safe, n + 1)
                    dve.wait_ge(pow_ready, n + 1)
                    refine(v, y, newton[:, 1, :], newton[:, 2, :])
                    link(nc.vector.scalar_tensor_tensor(out=rscale[:, cols], in0=deg[:, cols], scalar=0.0, in1=y,
                                                        op0=ALU.is_gt, op1=ALU.mult))
                    for j in range(n * TPS, (n + 1) * TPS):
                        last = nc.vector.tensor_scalar(feats_rows[:, j, :], feats_rows[:, j, :], mv[:, j, 0:1],
                                                       rscale[:, j:j + 1], ALU.subtract, ALU.mult)
                    link(last)
                    rows = feats_rows[:, cols, :]
                    link(nc.vector.tensor_copy(xs[:, cols, 0, :], rows))
                    nc.vector.tensor_tensor(xs[:, cols, 1, :], rows, xs[:, cols, 0, :],
                                            ALU.subtract).then_inc(xs_ready, 1)
                elif n in rests:
                    add_group(n)

            v, y = newton_z[:, 0, :], newton_z[:, 3, :]
            nc.vector.tensor_scalar(v, deg[:, :], DEG_FLOOR, XS_SCALE ** 2, ALU.max, ALU.mult).then_inc(norm_safe, 1)
            dve.wait_ge(norm_safe, 1)
            dve.wait_ge(norm_pow, 1)
            refine(v, y, newton_z[:, 1, :], newton_z[:, 2, :])
            link(nc.vector.scalar_tensor_tensor(out=dis_down[:, :], in0=deg[:, :], scalar=0.0, in1=y,
                                                op0=ALU.is_gt, op1=ALU.mult))
            dve.wait_ge(weights_in, 16 * 6)
            nc.vector.tensor_copy(earlier[:, :], con[:, 0:P]).then_inc(consts_cast, 1)
            nc.vector.memset(all_ones[:, :], 1.0).then_inc(consts_cast, 1)
            for e in range(E):
                dve.wait_ge(w1_high, e + 1)
                nc.vector.scalar_tensor_tensor(out=w1s[:, e, 1], in0=w1_in_sb[:, e % 2, :].rearrange("p (k n) -> p k n", k=KD),
                                               scalar=W_SCALE, in1=w1s[:, e, 0], op0=ALU.mult,
                                               op1=ALU.subtract).then_inc(w1_low, 1)
            iota_e = con[:, C_IOTA_E:C_IOTA_E + E]
            iota_t = con[:, C_IOTA_T:C_IOTA_T + SLOT_TILES]
            before = con[:, C_BEFORE:C_BEFORE + E * E].rearrange("p (a b) -> p a b", a=E)
            for kind, k in ending():
                if kind == "groups":
                    for g in last_groups[k]:
                        if g in rests:
                            add_group(g)
                elif kind == "z":
                    linear_and_norm(k)
                elif kind == "g":
                    top_two(k)
                elif kind == "route":
                    route(k)
            for e in range(E):
                dve.wait_ge(w2_high, e + 1)
                nc.vector.scalar_tensor_tensor(out=w2s[:, e, 1].rearrange("p k d -> p (k d)"),
                                               in0=w2_in_sb[:, e * KF * D:(e + 1) * KF * D], scalar=W_SCALE,
                                               in1=w2s[:, e, 0].rearrange("p k d -> p (k d)"), op0=ALU.mult,
                                               op1=ALU.subtract).then_inc(w2_low, 1)

            def xT_low_part(n, parity):
                dve.wait_ge(xT_high, n + 1)
                nc.vector.tensor_tensor(xT_parts[:, parity, 1].rearrange("p k n -> p (k n)"), degree[parity][:, 0:D],
                                        xT_parts[:, parity, 0].rearrange("p k n -> p (k n)"),
                                        ALU.subtract).then_inc(xT_low, 1)

            def split_hidden(n, parity):
                dve.wait_ge(h_relu, n + 1)
                dve.wait_ge(y_summed, n - 1 + AHEAD)
                nc.vector.tensor_copy(h_parts[:, parity, 0], h_sb[:, parity]).then_inc(h_high, 1)
                dve.wait_ge(h_high, n + 1)
                nc.vector.tensor_tensor(h_parts[:, parity, 1], h_sb[:, parity], h_parts[:, parity, 0],
                                        ALU.subtract).then_inc(h_low, 1)

            def expert_out(n, parity, stored, e):
                dve.wait_ge(y_summed, n + 1 + AHEAD)
                dve.wait_ge(y_stored[parity], stored)
                nc.vector.scalar_tensor_tensor(
                    out=y_sb[:, parity, :], in0=banks[2 + parity][:, 0:D], scalar=1.0 / W_SCALE,
                    in1=b2_rows[:, bass.ds(e, 1), :].rearrange("p a d -> p (a d)"),
                    op0=ALU.mult, op1=ALU.add).then_inc(y_ready, 1)

            dve.wait_ge(b2_in, 16)
            dve.sem_inc(h_low, AHEAD)
            dve.sem_inc(y_ready, AHEAD)
            for part in range(PARTS):
                first = part * SLOT_TILES
                xT_low_part(first, first % 2)
                xT_low_part(first + 1, (first + 1) % 2)
                split_hidden(first, first % 2)
                with dve.Fori(0, TURNS) as turn:
                    es = experts_of(dve, part, turn * UNROLL, UNROLL)
                    for u in range(UNROLL):
                        n = turn * UNROLL + u + first
                        xT_low_part(n + 2, (first + u) % 2)
                        split_hidden(n + 1, (first + u + 1) % 2)
                        expert_out(n, (first + u) % 2, turn * (16 * UNROLL // 2) + 16 * ((first + u) // 2 + 1), es[u])
                for tile in range(TURNS * UNROLL, SLOT_TILES):
                    n = first + tile
                    if tile + 2 < SLOT_TILES:
                        xT_low_part(n + 2, n % 2)
                    if tile + 1 < SLOT_TILES:
                        split_hidden(n + 1, (n + 1) % 2)
                    expert_out(n, n % 2, 16 * (n // 2 + 1), expert_of(dve, part, tile))

            for k in range(NSB):
                part = k // KPP
                dve.wait_ge(fetched[k], 16 * TPS * TOP)
                for r in range(TOP):
                    for j in range(TPS):
                        t = k % KPP * TPS + j
                        row = feats_rows[:, ORDER[k] * TPS + j, :]
                        last = nc.vector.scalar_tensor_tensor(
                            out=row, in0=gathered[part][:, t, r, :], scalar=pair_w[:, part, r, t:t + 1], in1=row,
                            op0=ALU.mult, op1=ALU.add)
                    if r < TOP - 1:
                        link(last)
                last.then_inc(summed_out, 1)

        @block.tensor
        def _(pe):
            def product_group(n):
                b, i, half, c0, c1 = groups[n]
                pe.wait_ge(xs_ready, b + 1)
                if n >= PSUM_GROUPS:
                    wait_evacuated(pe, n - PSUM_GROUPS)
                tiles = range(c0 * TPS, c1 * TPS)
                for j in tiles:
                    for part in range(2):
                        last = nc.tensor.matmul(
                            banks[n % PSUM_GROUPS][:, :], xs[:, j, part, half * P:(half + 1) * P],
                            a8[:, slots[i, j // TPS], j % TPS * SB:(j % TPS + 1) * SB],
                            start=(j == tiles[0] and part == 0), stop=(j == tiles[-1] and part == 1))
                last.then_inc(group_done, 1)

            pe.wait_ge(ident_made, 4)
            for kind, n in tensor_order:
                if kind == "piece":
                    pe.wait_ge(piece_cast, n + 1)
                    b, p = divmod(n, PPS)
                    if p == 0 and b >= 2:
                        pe.wait_ge(deg_read, b - 1)
                    for k in range(PIECE_TILES):
                        for i in range(TPS):
                            last = nc.tensor.matmul(
                                degree[b % 2][:, i:i + 1], a8_piece(n)[:, k * SB + i * P:k * SB + (i + 1) * P], ones8[:, :],
                                start=(p == 0 and k == 0 and i == 0), stop=(p == PPS - 1 and k == PIECE_TILES - 1),
                                skip_group_check=True)
                    last.then_inc(deg_summed, 1)
                else:
                    product_group(n)

            pe.wait_ge(weights_in, 16 * 6)
            pe.wait_ge(consts_cast, 2)
            for kind, k in ending():
                if kind == "groups":
                    for g in last_groups[k]:
                        product_group(g)
                elif kind == "z":
                    i = ORDER[k]
                    for g in last_groups[k]:
                        wait_evacuated(pe, g)
                    if k == 0:
                        pe.wait_ge(deg_read, NSB)
                    else:
                        pe.wait_ge(z_used, k)
                    for j in range(TPS):
                        for half in range(KD):
                            last = nc.tensor.matmul(degree[j // 2][:, j % 2 * D:(j % 2 + 1) * D],
                                                    feats_cols[:, i, half, j * P:(j + 1) * P], wT[:, half, :],
                                                    start=half == 0, stop=half == KD - 1)
                    last.then_inc(z_done, 1)
                elif kind == "t":
                    pe.wait_ge(normed_ready, k + 1)
                    if k:
                        pe.wait_ge(turned_out, k)
                    for half in range(KD):
                        for j in range(TPS):
                            last = nc.tensor.transpose(banks[4 + half][:, j * P:(j + 1) * P],
                                                       normed(k)[:, j, half * P:(half + 1) * P], ident[:, :])
                    last.then_inc(turned, 1)
                elif kind == "g":
                    pe.wait_ge(turned_out, k + 1)
                    if k:
                        pe.wait_ge(logits_read, k)
                    if k == KPP:
                        pe.wait_ge(rank_read, 1)
                    for j in range(TPS):
                        for half in range(KD):
                            last = nc.tensor.matmul(banks[3][:, j * E:(j + 1) * E], xT_gate[:, half, j * P:(j + 1) * P],
                                                    gate[:, half, :], start=half == 0, stop=half == KD - 1)
                    last.then_inc(gate_done, 1)
                else:
                    pe.wait_ge(masks_ready, k + 1)
                    pe.wait_ge(logits_read, KPP * (k + 1))
                    flat = mask_sum[:, :, :].rearrange("p t e -> p (t e)")
                    nc.tensor.matmul(banks[3][:, 0:TPP * E], earlier[:, :], flat, start=True, stop=False,
                                     skip_group_check=True)
                    for t in range(1, TPP):
                        nc.tensor.matmul(banks[3][:, t * E:TPP * E], all_ones[:, :], flat[:, 0:(TPP - t) * E],
                                         start=False, stop=t == TPP - 1, skip_group_check=True)
                    for t in range(TPP):
                        last = nc.tensor.matmul(banks[3][:, TPP * E:(TPP + 1) * E], all_ones[:, :], mask_sum[:, t, :],
                                                start=False, stop=t == TPP - 1, skip_group_check=True)
                    last.then_inc(ranked, 1)

            def turn_rows(n, slot, loads, parity):
                pe.wait_ge(sorted_load[slot], loads)
                for half in range(KD):
                    last = nc.tensor.transpose(degree[parity][:, half * P:(half + 1) * P],
                                               sorted_in[:, slot, half * P:(half + 1) * P], ident[:, :])
                last.then_inc(tile_turned, 1)

            def hidden(n, parity, e):
                pe.wait_ge(xT_low, n + 1)
                for f in range(KF):
                    for half in range(KD):
                        for x_part, w_part in ((0, 0), (1, 0), (0, 1)):
                            last = nc.tensor.matmul(
                                banks[parity][:, f * P:(f + 1) * P],
                                w1s[:, bass.ds(e, 1), w_part, half, f * P:(f + 1) * P].rearrange("p a n -> p (a n)"),
                                xT_parts[:, parity, x_part, half, :],
                                start=(half == 0 and x_part == w_part), stop=(half == KD - 1 and w_part == 1))
                last.then_inc(h_summed, 1)

            def down(n, parity, e):
                pe.wait_ge(h_low, n + 1 + AHEAD)
                pe.wait_ge(y_ready, n - 1 + AHEAD)
                for f in range(KF):
                    for h_part, w_part in ((0, 0), (0, 1), (1, 0)):
                        last = nc.tensor.matmul(
                            banks[2 + parity][:, 0:D], h_parts[:, parity, h_part, f, :],
                            w2s[:, bass.ds(e, 1), w_part, f, :].rearrange("p a n -> p (a n)"),
                            start=(f == 0 and h_part == w_part), stop=(f == KF - 1 and h_part == 1))
                last.then_inc(y_summed, 1)

            pe.wait_ge(w2_low, E)
            pe.wait_ge(slots_ready, PARTS)
            pe.sem_inc(h_summed, AHEAD)
            pe.sem_inc(y_summed, AHEAD)
            for part in range(PARTS):
                first = part * SLOT_TILES

                def at(tile):
                    n = first + tile
                    return n % 4, 16 * (n // 4 + 1), n % 2

                turn_rows(first, *at(0))
                turn_rows(first + 1, *at(1))
                hidden(first, first % 2, expert_of(pe, part, 0))
                with pe.Fori(0, TURNS) as turn:
                    es = experts_of(pe, part, turn * UNROLL, UNROLL + 1)
                    for u in range(UNROLL):
                        n = turn * UNROLL + u + first
                        slot, loads, parity = at(u + 2)
                        turn_rows(n + 2, slot, turn * 16 + loads, parity)
                        hidden(n + 1, 1 - parity, es[u + 1])
                        down(n, parity, es[u])
                for tile in range(TURNS * UNROLL, SLOT_TILES):
                    n = first + tile
                    if tile + 2 < SLOT_TILES:
                        turn_rows(n + 2, *at(tile + 2))
                    if tile + 1 < SLOT_TILES:
                        hidden(n + 1, (n + 1) % 2, expert_of(pe, part, tile + 1))
                    down(n, n % 2, expert_of(pe, part, tile))


def kernel(x, adj, L0_gnn_W, L0_gnn_b, L0_ffn_gate_w, L0_ffn_gate_b, L0_ffn_w1, L0_ffn_b1, L0_ffn_w2, L0_ffn_b2):
    import numpy as np
    import concourse.bacc as bacc
    from concourse.bass_utils import run_bass_kernel_spmd

    pieces = np.ascontiguousarray(np.asarray(adj).reshape(NSB, SB, PPS, PIECE_TILES, P).transpose(0, 2, 4, 3, 1))
    arrays = {
        "x": np.ascontiguousarray(x), "adj_pieces": pieces.reshape(PIECES, P, PIECE),
        "gnn_wT": np.ascontiguousarray(np.asarray(L0_gnn_W).T), "gnn_b": np.ascontiguousarray(L0_gnn_b).reshape(1, D),
        "gate_w": np.ascontiguousarray(L0_ffn_gate_w), "gate_b": np.ascontiguousarray(L0_ffn_gate_b).reshape(1, E),
        "w1": np.ascontiguousarray(L0_ffn_w1), "b1": np.ascontiguousarray(np.asarray(L0_ffn_b1).reshape(E, KF, P).transpose(2, 0, 1)),
        "w2": np.ascontiguousarray(L0_ffn_w2), "b2": np.ascontiguousarray(L0_ffn_b2).reshape(E * D),
    }
    con = np.zeros((P, NCONST), np.float32)
    con[:, 0:P] = np.triu(np.ones((P, P)), 1)
    con[:, C_IOTA_E:C_IOTA_E + E] = np.arange(E)
    con[:, C_IOTA_T:C_IOTA_T + SLOT_TILES] = np.arange(SLOT_TILES)
    con[:, C_BEFORE:] = P * np.tril(np.ones((E, E)), -1).reshape(-1)
    arrays["consts"] = con
    nc = bacc.Bacc("TRN2", target_bir_lowering=False, num_devices=1)
    ins = [nc.dram_tensor(name, a.shape, mybir.dt.from_np(a.dtype), kind="ExternalInput").ap()
           for name, a in arrays.items()]
    out = nc.dram_tensor("out", (N, D), mybir.dt.float32, kind="ExternalOutput").ap()
    build(nc, *ins, out)
    r = run_bass_kernel_spmd(nc, [arrays], core_ids=[0])
    return r.results[0]["out"]
```

```python
from contextlib import ExitStack

import concourse.bass as bass
from concourse import mybir

N, D = 4096, 256
E, F = 8, 512
P = 128
SB = 512
NSB = N // SB
NT = N // P
TPS = SB // P
KD = D // P
KF = F // P
PIECE_TILES = 2
PIECES = NT // PIECE_TILES * NSB
PPS = PIECES // NSB
PIECE = PIECE_TILES * SB
STAGES = 7
F_STAGES = 4
PSUM_GROUPS = 3
XS_SCALE = 128.0
W_SCALE = 64.0
EPS = 1e-5
ORDER = [NSB - 1] + list(range(NSB - 1))
TOP = 2
ROWS = 2 * P
MT = N * TOP // ROWS + E - 1
W = D + 2
C_IOTA_E = P
C_IOTA_T = C_IOTA_E + E
C_BEFORE = C_IOTA_T + MT
C_TOKEN = C_BEFORE + E * E
NCONST = C_TOKEN + NT + 2
UNROLL = 8
TURNS = (MT - 3) // UNROLL
AHEAD = 2
RING = UNROLL
LANDED = 4
DEG_FLOOR = 2.0 ** -10


def adjacency_slots():
    kept = sorted(((b, c) for b in range(NSB - 2) for c in range(NSB)), key=lambda k: (max(k), k))
    slots = {k: n for n, k in enumerate(kept)}
    for b in (NSB - 2, NSB - 1):
        for c in range(NSB):
            slots[b, c] = (b - (NSB - 2)) * NSB + c
    return slots, len(kept)


def timeline():
    groups = []
    for b in range(NSB):
        groups += [(b, b, half, 0, b + 1) for half in range(KD)]
        groups += [(b, i, half, b, b + 1) for i in range(b) for half in range(KD)]
    arrive = [5.0 + 1.8 * (n + 1) for n in range(PIECES)]
    tensor, timed = [], [(arrive[n], 0, ("piece", n)) for n in range(PIECES)]
    timed += [(arrive[PPS * b + 6], 0, ("norm", b)) for b in range(NSB)]
    count_time = arrive[-1] + 6.0
    timed += [(count_time, 3, ("count", 0)), (arrive[-1] + 8.0, 3, ("down", 0)), (arrive[-1] + 16.0, 3, ("down", 1))]
    now, piece, counted = 0.0, 0, False
    scaled = [0.0] * NSB
    for b in range(NSB):
        for g, (step, i, half, c0, c1) in enumerate(groups):
            if step != b:
                continue
            while piece < PIECES and (piece < PPS * (b + 1) or arrive[piece] <= now):
                now = max(now, arrive[piece]) + 0.3
                tensor.append(("piece", piece))
                piece += 1
                if piece % PPS == 0:
                    timed.append((now, 1, ("prep", piece // PPS - 1)))
                    scaled[piece // PPS - 1] = now + 4.5
            if piece == PIECES and now > count_time and not counted:
                counted = True
                tensor.append(("count", 0))
                timed.append((now + 1.0, 3, ("flag", 0)))
            tensor.append(("group", g))
            now = max(now, scaled[b]) + 1.75 * (c1 - c0)
            timed.append((now, 2, ("group", g)))
    last = [g for g, k in enumerate(groups) if k[0] == NSB - 1]
    tensor = [event for event in tensor if event not in [("group", g) for g in last]]
    timed = [event for _, _, event in sorted(timed) if event not in [("group", g) for g in last]]
    return groups, tensor, timed


def ending():
    order = []
    for k in range(NSB + 3):
        if k < NSB:
            order.append(("groups", k))
        for kind, lag in (("z", 1), ("t", 2), ("g", 3)):
            if 0 <= k - lag < NSB:
                order.append((kind, k - lag))
    return order + [("route", 0)]


def build(nc, x, adj_pieces, gnn_wT, gnn_b, gate_w, gate_b, w1, b1, w2, b2, consts, out):
    f32, f16, f8, bf16 = mybir.dt.float32, mybir.dt.float16, mybir.dt.float8e4, mybir.dt.bfloat16
    i32, u32 = mybir.dt.int32, mybir.dt.uint32
    ALU = mybir.AluOpType
    ACT = mybir.ActivationFunctionType
    AXX = mybir.AxisListType.X
    groups, tensor_order, vector_order = timeline()
    slots, nslots = adjacency_slots()
    ng = len(groups)
    last_groups = {k: [g for g, (b, i, *_) in enumerate(groups) if b == NSB - 1 and i == ORDER[k]]
                   for k in range(NSB)}

    ctx = ExitStack()
    with ctx:
        def sb(name, shape, dt):
            return ctx.enter_context(nc.sbuf_tensor(name, shape, dt))

        def sem(name):
            return ctx.enter_context(nc.semaphore(name))

        feats = sb("feats", [P, NSB, TPS * D], f32)
        xs = sb("xs", [P, NT, 2, D], f16)
        pool_words = sb("pool_words", [P, nslots * SB + NT * W - NT * D], f32)
        a8 = pool_words[:, 0:nslots * SB].bitcast(f8).rearrange("p (s n) -> p s n", s=nslots)
        stage = sb("stage", [P, STAGES, PIECE], f32)
        scratch = sb("scratch", [P, 256], f32)
        unequal = sb("unequal", [P, 2, PIECE], mybir.dt.bfloat16)
        mism = sb("mism", [P, PIECES], f32)
        ones32 = sb("ones32", [P, 1], f32)
        found = sb("found", [P, 1], f32)
        inexact = sb("inexact", [P, 1], i32)
        ident = sb("ident", [P, P], f32)
        ones8 = sb("ones8", [P, 1], f8)
        stats = sb("stats", [P, TPS, 6], f32)
        stats_z = sb("stats_z", [P, TPS, 6], f32)
        mv_z = sb("mv_z", [P, TPS, 2], f32)
        newton_z = sb("newton_z", [P, 4, NT], f32)
        mv = sb("mv", [P, NT, 2], f32)
        newton = sb("newton", [P, 4, TPS], f32)
        minus_half = sb("minus_half", [P, NT], f32)
        var = sb("var", [P, NT], f32)
        deg = sb("deg", [P, NT], f32)
        rscale = sb("rscale", [P, NT], f32)

        dis_down = sb("dis_down", [P, NT], f32)
        wT = sb("wT", [P, KD, D], f32)
        bias_rows = sb("bias_rows", [P, D], f32)
        gate = sb("gate", [P, KD, E], f32)
        gate_bias = sb("gate_bias", [P, E], f32)
        b1_cols = sb("b1_cols", [P, E, KF], f32)
        blank = sb("blank", [P, 2, W], f32)
        con = sb("con", [P, NCONST], f32)
        earlier = sb("earlier", [P, P], bf16)
        all_ones = sb("all_ones", [P, P], bf16)
        mask_sum = sb("mask_sum", [P, NT, E], bf16)
        idxf = sb("idxf", [P, TOP, NT], f32)
        counts_i = sb("counts_i", [P, 2, E], i32)
        tiles_f = sb("tiles_f", [P, E], f32)
        prod8 = sb("prod8", [P, E, E], f32)
        base = sb("base", [P, E], f32)
        ends = sb("ends", [P, E], f32)
        over = scratch[:, :].bitcast(bf16)[:, 0:MT * E].rearrange("p (t e) -> p t e", e=E)
        owner = sb("owner", [P, MT], f32)
        slot_f = sb("slot_f", [P, TOP, NT], f32)
        top_gap = sb("top_gap", [P, NT], f32)
        exp_gap = sb("exp_gap", [P, NT], f32)
        denom = sb("denom", [P, NT], f32)
        slot_of = sb("slot_of", [P, TOP, NT], u32)
        pair_w = sb("pair_w", [P, TOP, NT], f32)
        tile_e = sb("tile_e", [P, -(-MT // 8) * 8], i32)

        def words(first_slot, slots_):
            return pool_words[:, first_slot * SB:(first_slot + slots_) * SB]

        w2s = words(0, 16).bitcast(f16).rearrange("p (e s k n) -> p e s k n", e=E, s=2, k=KF)
        w1s = words(16, 16).bitcast(f16).rearrange("p (e s k n) -> p e s k n", e=E, s=2, k=KD)
        rows_out = pool_words[:, 32 * SB:32 * SB + NT * W].rearrange("p (t w) -> p t w", w=W)
        xs_words = xs[:, :, :, :].rearrange("p t s d -> p (t s d)").bitcast(f32)
        w2_in_sb = xs_words
        logits = stage[:, 0, 0:NT * E].rearrange("p (t e) -> p t e", e=E)
        top8 = stage[:, 0, NT * E:2 * NT * E].rearrange("p (t e) -> p t e", e=E)
        idx8 = stage[:, 0, 2 * NT * E:3 * NT * E].bitcast(u32).rearrange("p (t e) -> p t e", e=E)
        rank = stage[:, 0, 3 * NT * E:4 * NT * E].rearrange("p (t e) -> p t e", e=E)
        mask = stage[:, 1, 0:TOP * NT * E].rearrange("p (r t e) -> p r t e", r=TOP, e=E)
        picked = stage[:, 1, TOP * NT * E:(TOP + 1) * NT * E].rearrange("p (t e) -> p t e", e=E)
        x_again = [stage[:, 2 + n, :].rearrange("p (t d) -> p t d", d=D) for n in range(2)]
        w1_in_sb = stage[:, 4:6, :]
        xT_gate = stage[:, 6, :].rearrange("p (k n) -> p k n", k=KD)
        feats_words = feats[:, :, :].rearrange("p b n -> p (b n)")
        b2_rows = feats_words[:, 0:E * D].rearrange("p (e d) -> p e d", e=E)
        y_sb = feats_words[:, E * D:E * D + 4 * D].rearrange("p (r s d) -> p r s d", r=2, s=2)
        sorted_in = feats_words[:, E * D + 4 * D:E * D + 4 * D + RING * 2 * W].rearrange("p (r s w) -> p r s w", r=RING, s=2)
        xT_parts = xs_words[:, 0:2 * KD * ROWS].bitcast(f16).rearrange("p (r s k n) -> p r s k n", r=2, s=2, k=KD)
        h_sb = xs_words[:, 1024:1024 + 2 * KF * ROWS].rearrange("p (r k n) -> p r k n", r=2, k=KF)
        h_parts = xs_words[:, 3072:3072 + 2 * KF * ROWS].bitcast(f16).rearrange("p (r s k n) -> p r s k n", r=2, s=2, k=KF)

        def normed(k):
            return rows_out[:, k * TPS:(k + 1) * TPS, 0:D]

        x_sorted = nc.dram_tensor("x_sorted", (MT * ROWS, W), f32).ap()

        degree = [ctx.enter_context(nc.psum_tensor(f"degree{n}", [P, 512], f32)) for n in range(2)]
        banks = [ctx.enter_context(nc.psum_tensor(f"bank{n}", [P, 512], f32)) for n in range(6)]

        x_in = sem("x_in")

        adj_in = [sem(f"adj_in{n}") for n in range(STAGES)]
        last_cleared = sem("last_cleared")
        found_ready = sem("found_ready")
        found_summed = sem("found_summed")
        inexact_ready = sem("inexact_ready")
        down_safe = sem("down_safe")
        down_pow = sem("down_pow")
        down_ready = sem("down_ready")
        f_x_in = sem("f_x_in")
        f_adj_in = [sem(f"f_adj_in{n}") for n in range(F_STAGES)]
        f_piece_used = sem("f_piece_used")
        f_deg_read = sem("f_deg_read")
        f_pow_safe = sem("f_pow_safe")
        f_pow_ready = sem("f_pow_ready")
        f_rows_ready = sem("f_rows_ready")
        f_stored = sem("f_stored")
        f_cleared = sem("f_cleared")
        f_turned = sem("f_turned")
        f_added = sem("f_added")
        f_chain = sem("f_chain")
        chain = sem("chain")
        ident_made = sem("ident_made")
        deg_read = sem("deg_read")
        pow_ready = sem("pow_ready")
        diag_added = sem("diag_added")
        piece_cast = sem("piece_cast")
        piece_checked = sem("piece_checked")
        piece_compared = sem("piece_compared")
        difference_summed = sem("difference_summed")
        deg_summed = sem("deg_summed")
        deg_safe = sem("deg_safe")
        xs_ready = sem("xs_ready")
        group_done = sem("group_done")
        first_stored = sem("first_stored")
        rest_added = sem("rest_added")
        weights_in = sem("weights_in")
        zeros_made = sem("zeros_made")
        rows_zeroed = sem("rows_zeroed")
        x_again_in = [sem(f"x_again_in{n}") for n in range(2)]
        w1_in = [sem(f"w1_in{n}") for n in range(2)]
        w1_high = sem("w1_high")
        w1_low = sem("w1_low")
        w2_in = sem("w2_in")
        w2_high = sem("w2_high")
        w2_low = sem("w2_low")
        b2_in = sem("b2_in")
        norm_safe = sem("norm_safe")
        norm_pow = sem("norm_pow")
        z_done = sem("z_done")
        z_used = sem("z_used")
        normed_ready = sem("normed_ready")
        turned = sem("turned")
        turned_out = sem("turned_out")
        gate_done = sem("gate_done")
        logits_read = sem("logits_read")
        masks_ready = sem("masks_ready")
        ranked = sem("ranked")
        rank_read = sem("rank_read")
        slots_ready = sem("slots_ready")
        gap_ready = sem("gap_ready")
        exp_ready = sem("exp_ready")
        pair_w_ready = sem("pair_w_ready")
        consts_cast = sem("consts_cast")
        scattered_first = [sem(f"scattered_first{n}") for n in range(NSB)]
        meta_ready = sem("meta_ready")
        second_weights = sem("second_weights")
        scattered = sem("scattered")
        sorted_load = [sem(f"sorted_load{n}") for n in range(RING)]
        tile_turned = sem("tile_turned")
        xT_high = sem("xT_high")
        xT_low = sem("xT_low")
        h_summed = sem("h_summed")
        h_relu = sem("h_relu")
        h_high = sem("h_high")
        h_low = sem("h_low")
        y_summed = sem("y_summed")
        y_ready = sem("y_ready")
        y_weighted = sem("y_weighted")
        landed = sem("landed")
        added = sem("added")
        out_sent = sem("out_sent")

        block = ctx.enter_context(nc.Block())
        x_tiles = x.rearrange("(t p) d -> p t d", p=P)
        out_tiles = out[0:N, :].rearrange("(t p) d -> p t d", p=P)
        feats_rows = feats[:, :, :].rearrange("p b (t d) -> p (b t) d", d=D)
        feats_cols = feats[:, :, :].rearrange("p b (h i) -> p b h i", h=KD)

        firsts = [g for g in range(ng) if groups[g][0] == groups[g][1] < NSB - 1]
        rests = [g for g in range(ng) if g not in firsts]
        streamed = [g for g in range(ng) if groups[g][0] < NSB - 1]

        def wait_evacuated(eng, g):
            if g in firsts:
                eng.wait_ge(first_stored, firsts.index(g) + 1)
            else:
                eng.wait_ge(rest_added, rests.index(g) + 1)

        def on_pool(n):
            return n % 8 in (2, 5, 7)

        def wait_checked(eng, n):
            mine = sum(on_pool(m) == on_pool(n) for m in range(n + 1))
            eng.wait_ge(piece_compared if on_pool(n) else piece_checked, mine)

        def a8_piece(n):
            b, q = divmod(n, PPS)
            c, half = divmod(q, TPS // PIECE_TILES)
            return a8[:, slots[b, c], half * PIECE:(half + 1) * PIECE]

        def expert_of(eng, tile):
            return eng.value_load(tile_e[0:1, bass.ds(tile, 1)], min_val=0, max_val=E - 1)

        def experts_of(eng, tile, count, name):
            registers = [eng.alloc_register(f"expert_{name}_{n}") for n in range(count)]
            eng.load(registers, tile_e[0:1, bass.ds(tile, count)])
            return [eng.snap(r, min_val=0, max_val=E - 1) for r in registers]

        def adj_arrived(eng, n):
            eng.wait_ge(adj_in[n % STAGES], 16 * (n // STAGES + 1))

        def diag_pieces(n):
            return sum(m // PPS == m % PPS * PIECE_TILES // TPS for m in range(n))

        f_rows = words(0, 16).rearrange("p (t d) -> p t d", d=D)

        def is_inexact(eng):
            eng.wait_ge(inexact_ready, 1)
            return eng.value_load(inexact[0:1, 0:1], min_val=0, max_val=P * PIECES) > 0

        def wait_steps_done(eng):
            eng.wait_ge(group_done, len(streamed))
            eng.wait_ge(first_stored, len(firsts))
            eng.wait_ge(rest_added, sum(g in streamed for g in rests))
            eng.wait_ge(xs_ready, NSB)
            eng.wait_ge(last_cleared, 1)
            eng.wait_ge(down_ready, 1)
            eng.wait_ge(deg_summed, PIECES)

        def f_load(sp):
            wait_steps_done(sp)
            sp.dma_start(f_rows, x_tiles).then_inc(f_x_in, 16)
            for sweep in range(2):
                with sp.Fori(0, NSB) as b:
                    for q in range(PPS):
                        sp.wait_ge(f_piece_used, b * PPS + (sweep * PIECES + q + 1))
                        sp.dma_start(stage[:, q % F_STAGES, :],
                                     adj_pieces[bass.ds(b * PPS + q, 1)].rearrange("a p n -> (a p) n")
                                     ).then_inc(f_adj_in[q % F_STAGES], 16)
            sp.wait_ge(f_cleared, 2)

        def f_power(pool):
            for n in range(2):
                pool.wait_ge(f_pow_safe, n + 1)
                nc.gpsimd.tensor_tensor(newton_z[:, 3, :], newton_z[:, 0, :], minus_half[:, :],
                                        ALU.pow).then_inc(f_pow_ready, 1)
            pool.wait_ge(f_cleared, 2)

        def f_store(act):
            with act.Fori(0, NSB) as b:
                act.wait_ge(f_piece_used, b * PPS + (F_STAGES + PIECES + PPS))
                for half in range(KD):
                    last = nc.scalar.activation(
                        feats[:, bass.ds(b, 1), half * SB:(half + 1) * SB].rearrange("p a n -> p (a n)"),
                        banks[half][:, :], ACT.Copy)
                last.then_inc(f_stored, 1)
            act.wait_ge(f_cleared, 2)

        def f_scale(dve):
            links = [0]

            def link(ins):
                links[0] += 1
                ins.then_inc(f_chain, 1)
                dve.wait_ge(f_chain, links[0])

            def refine(v, y, t, u):
                link(nc.vector.tensor_tensor(t, y, y, ALU.mult))
                link(nc.vector.tensor_tensor(u, t, v, ALU.mult))
                link(nc.vector.tensor_scalar(t, u, -0.5, 1.5, ALU.mult, ALU.add))
                link(nc.vector.tensor_tensor(y, y, t, ALU.mult))

            wait_steps_done(dve)
            with dve.Fori(0, NSB) as b:
                dve.wait_ge(f_piece_used, b * PPS + (F_STAGES + PPS))
                nc.vector.tensor_scalar(deg[:, bass.ds(b * TPS, TPS)], degree[0][:, 0:TPS], 1.0, None,
                                        ALU.add).then_inc(f_deg_read, 1)
            dve.wait_ge(f_deg_read, NSB + 1)
            v, t, u, y = (newton_z[:, n, :] for n in range(4))
            nc.vector.tensor_scalar(v, deg[:, :], 1e-37, 1e38, ALU.max, ALU.min).then_inc(f_pow_safe, 1)
            dve.wait_ge(f_pow_safe, 1)
            dve.wait_ge(f_pow_ready, 1)
            refine(v, y, t, u)
            link(nc.vector.scalar_tensor_tensor(out=dis_down[:, :], in0=deg[:, :], scalar=0.0, in1=y,
                                                op0=ALU.is_gt, op1=ALU.mult))
            nc.vector.tensor_scalar(v, mv[:, :, 1], EPS, None, ALU.add).then_inc(f_pow_safe, 1)
            dve.wait_ge(f_pow_safe, 2)
            dve.wait_ge(f_pow_ready, 2)
            refine(v, y, t, u)
            link(nc.vector.tensor_tensor(rscale[:, :], y, dis_down[:, :], ALU.mult))
            dve.wait_ge(f_x_in, 16)
            for j in range(NT):
                last = nc.vector.tensor_scalar(f_rows[:, j, :], f_rows[:, j, :], mv[:, j, 0:1], rscale[:, j:j + 1],
                                               ALU.subtract, ALU.mult)
            last.then_inc(f_rows_ready, 1)
            dve.wait_ge(f_stored, NSB + 1)
            for b in range(NSB):
                dve.wait_ge(f_turned, b + 1)
                for half in range(KD):
                    last = nc.vector.tensor_tensor(feats_cols[:, b, half, :], feats_cols[:, b, half, :],
                                                   banks[2 + half][:, :], ALU.add)
                last.then_inc(f_added, 1)
            dve.wait_ge(f_added, NSB)
            nc.vector.memset(xs[:, :, :, :].rearrange("p t s d -> p (t s d)").bitcast(f32), 0.0).then_inc(f_cleared, 1)
            nc.vector.memset(pool_words[:, 0:nslots * SB], 0.0).then_inc(f_cleared, 1)
            dve.wait_ge(f_cleared, 2)

        def f_products(pe):
            def piece(sweep, b, q):
                pe.wait_ge(f_adj_in[q % F_STAGES], b * (16 * PPS // F_STAGES) +
                           16 * (sweep * PIECES // F_STAGES + q // F_STAGES + 1))
                return stage[:, q % F_STAGES, :].rearrange("p (k n) -> p k n", k=PIECE_TILES)

            wait_steps_done(pe)
            pe.sem_inc(f_piece_used, F_STAGES)
            pe.sem_inc(f_deg_read, 1)
            pe.sem_inc(f_stored, 1)
            with pe.Fori(0, NSB) as b:
                pe.wait_ge(f_deg_read, b + 1)
                for q in range(PPS):
                    a = piece(0, b, q)
                    for k in range(PIECE_TILES):
                        for i in range(TPS):
                            last = nc.tensor.matmul(degree[0][:, i:i + 1], a[:, k, i * P:(i + 1) * P], ones32[:, :],
                                                    start=(q == 0 and k == 0 and i == 0),
                                                    stop=(q == PPS - 1 and k == PIECE_TILES - 1), skip_group_check=True)
                    last.then_inc(f_piece_used, 1)
            pe.wait_ge(f_rows_ready, 1)
            with pe.Fori(0, NSB) as b:
                pe.wait_ge(f_stored, b + 1)
                for q in range(PPS):
                    a = piece(1, b, q)
                    for k in range(PIECE_TILES):
                        for half in range(KD):
                            last = nc.tensor.matmul(banks[half][:, :], f_rows[:, q * PIECE_TILES + k, half * P:(half + 1) * P],
                                                    a[:, k, :], start=(q == 0 and k == 0), stop=(q == PPS - 1 and k == PIECE_TILES - 1))
                    last.then_inc(f_piece_used, 1)
            for b in range(NSB):
                if b:
                    pe.wait_ge(f_added, b)
                for half in range(KD):
                    for i in range(TPS):
                        last = nc.tensor.transpose(banks[2 + half][:, i * P:(i + 1) * P],
                                                   f_rows[:, b * TPS + i, half * P:(half + 1) * P], ident[:, :])
                last.then_inc(f_turned, 1)
            pe.wait_ge(f_cleared, 2)

        @block.sync
        def _(sp):
            for n in range(PIECES):
                if n >= STAGES:
                    wait_checked(sp, n - STAGES)
                    sp.wait_ge(piece_cast, n - STAGES + 1)
                sp.dma_start(stage[:, n % STAGES, :], adj_pieces[n]).then_inc(adj_in[n % STAGES], 16)
            with sp.If(is_inexact(sp)):
                f_load(sp)
            for e in range(E):
                if e >= 2:
                    sp.wait_ge(w1_low, e - 1)
                sp.dma_start(w1_in_sb[:, e % 2, :].rearrange("p (k f) -> p k f", k=KD),
                             w1[e].rearrange("(k p) f -> p k f", p=P)).then_inc(w1_in[e % 2], 16)
            sp.wait_ge(group_done, ng)
            for e in range(E):
                sp.dma_start(w2_in_sb.rearrange("p (e k d) -> p e k d", e=E, k=KF)[:, e],
                             w2[e].rearrange("(k p) d -> p k d", p=P)).then_inc(w2_in, 16)
            sp.wait_ge(out_sent, 16 * (NSB + 1))
            sp.wait_ge(normed_ready, NSB)
            sp.dma_start(b2_rows.rearrange("p e d -> p (e d)"), b2.partition_broadcast(P)).then_inc(b2_in, 16)

            for k in range(NSB):
                sp.wait_ge(scattered_first[k], 16 * TPS)
            sp.wait_ge(scattered, 16 * NT)
            sp.sem_inc(landed, LANDED)

            def load_rows(tile, slot):
                sp.dma_start(sorted_in[:, slot], x_sorted[bass.ds(tile * ROWS, ROWS), :].rearrange("(p s) w -> p s w", s=2)
                             ).then_inc(sorted_load[slot], 16)

            for tile in range(3):
                load_rows(tile, tile)
            with sp.Fori(0, TURNS) as turn:
                for u in range(UNROLL):
                    sp.wait_ge(landed, turn * UNROLL + (u + 1))
                    load_rows(turn * UNROLL + (u + 3), (u + 3) % RING)
            for tile in range(TURNS * UNROLL, MT - 3):
                sp.wait_ge(landed, tile + 1)
                load_rows(tile + 3, (tile + 3) % RING)

        @block.gpsimd
        def _(pool):
            nc.gpsimd.memset(blank[:, :, :], 0.0).then_inc(zeros_made, 1)
            nc.gpsimd.memset(minus_half[:, :], -0.5).then_inc(ident_made, 1)
            nc.gpsimd.memset(ident[:, :], 0.0).then_inc(ident_made, 1)
            nc.gpsimd.memset(ones8[:, :], 1.0).then_inc(ident_made, 1)
            nc.gpsimd.memset(ones32[:, :], 1.0).then_inc(ident_made, 1)
            pool.wait_ge(ident_made, 4)
            nc.gpsimd.affine_select(out=ident[:, :], in_=ident[:, :], compare_op=ALU.not_equal, fill=1.0,
                                    base=0, pattern=[[-1, P]], channel_multiplier=1).then_inc(ident_made, 1)
            pool.wait_ge(ident_made, 5)
            for kind, n in vector_order:
                if kind == "piece" and diag_pieces(n + 1) > diag_pieces(n):
                    adj_arrived(pool, n)
                    first = n % PPS * PIECE_TILES % TPS * P
                    for t in range(PIECE_TILES):
                        part = stage[:, n % STAGES, t * SB + first + t * P:t * SB + first + (t + 1) * P]
                        last = nc.gpsimd.tensor_tensor(part, part, ident[:, :], ALU.add)
                    last.then_inc(diag_added, 1)
                if kind == "piece" and on_pool(n):
                    pool.wait_ge(piece_cast, n + 1)
                    done = sum(on_pool(m) for m in range(n))
                    if done >= 2:
                        pool.wait_ge(difference_summed, done - 1)
                    nc.gpsimd.tensor_tensor(unequal[:, done % 2, :], stage[:, n % STAGES, :], a8_piece(n),
                                            ALU.subtract).then_inc(piece_compared, 1)
                if kind == "prep":
                    pool.wait_ge(deg_safe, n + 1)
                    nc.gpsimd.tensor_tensor(newton[:, 3, 0:TPS], newton[:, 0, 0:TPS], minus_half[:, 0:TPS],
                                            ALU.pow).then_inc(pow_ready, 1)
                if kind == "down" and n == 0:
                    pool.wait_ge(down_safe, 1)
                    nc.gpsimd.tensor_tensor(newton_z[:, 3, :], newton_z[:, 0, :], minus_half[:, :],
                                            ALU.pow).then_inc(down_pow, 1)
                    pool.wait_ge(xs_ready, NSB)
                    nc.gpsimd.memset(feats[:, NSB - 1, :], 0.0).then_inc(last_cleared, 1)
            with pool.If(is_inexact(pool)):
                f_power(pool)

            def power(n, width):
                pool.wait_ge(norm_safe, n + 1)
                nc.gpsimd.tensor_tensor(newton_z[:, 3, 0:width], newton_z[:, 0, 0:width], minus_half[:, 0:width],
                                        ALU.pow).then_inc(norm_pow, 1)

            for k in range(NSB):
                power(k, TPS)

            pool.wait_ge(rows_zeroed, 16)
            pool.wait_ge(slots_ready, 1)
            pool.wait_ge(meta_ready, 2)
            for r in range(TOP):
                for t in range(NT):
                    if r and t % TPS == 0:
                        pool.wait_ge(second_weights, t // TPS + 1)
                    nc.gpsimd.indirect_dma_start(
                        out=x_sorted[:, :], out_offset=bass.IndirectOffsetOnAxis(ap=slot_of[:, r, t:t + 1], axis=0),
                        in_=rows_out[:, t, :], in_offset=None).then_inc(scattered if r else scattered_first[t // TPS], 16)

            def add_rows(parity, slot):
                for s in range(2):
                    nc.gpsimd.indirect_dma_start(
                        out=out[:, :],
                        out_offset=bass.IndirectOffsetOnAxis(ap=sorted_in[:, slot, s, D + 1:D + 2].bitcast(u32), axis=0),
                        in_=y_sb[:, parity, s, :], in_offset=None, compute_op=ALU.add).then_inc(added, 16)

            pool.wait_ge(out_sent, 16 * (NSB + 1))
            pool.wait_ge(y_weighted, 1)
            pool.sem_inc(landed, 1)
            add_rows(0, 0)
            with pool.Fori(0, TURNS) as turn:
                for u in range(UNROLL):
                    pool.wait_ge(y_weighted, turn * UNROLL + (u + 2))
                    pool.wait_ge(added, turn * (32 * UNROLL) + 32 * (u + 1))
                    pool.sem_inc(landed, 1)
                    add_rows((u + 1) % 2, (u + 1) % RING)
            for tile in range(TURNS * UNROLL + 1, MT):
                pool.wait_ge(y_weighted, tile + 1)
                pool.wait_ge(added, 32 * tile)
                pool.sem_inc(landed, 1)
                add_rows(tile % 2, tile % RING)
            pool.wait_ge(added, 32 * MT)

        @block.scalar
        def _(act):
            def sum_difference(n):
                done = sum(on_pool(k) for k in range(n))
                act.wait_ge(piece_compared, done + 1)
                part = unequal[:, done % 2, :]
                nc.scalar.activation(part, part, ACT.Abs, accum_out=mism[:, n:n + 1]).then_inc(difference_summed, 1)

            def load_x_again(k):
                act.dma_start(x_again[k % 2], x_tiles[:, ORDER[k] * TPS:(ORDER[k] + 1) * TPS, :]).then_inc(x_again_in[k % 2], 16)

            def store_first(g):
                _, i, half, _, _ = groups[g]
                act.wait_ge(group_done, g + 1)
                nc.scalar.activation(feats_cols[:, i, half, :], banks[g % PSUM_GROUPS][:, :],
                                     ACT.Copy).then_inc(first_stored, 1)

            act.dma_start(feats_rows, x_tiles).then_inc(x_in, 16)
            for target, source in ((wT[:, :, :], gnn_wT.rearrange("(k p) n -> p k n", p=P)),
                                   (bias_rows[:, :], gnn_b[0, :].partition_broadcast(P)),
                                   (gate[:, :, :], gate_w.rearrange("(k p) e -> p k e", p=P)),
                                   (gate_bias[:, :], gate_b[0, :].partition_broadcast(P)),
                                   (b1_cols[:, :, :], b1), (con[:, :], consts)):
                act.dma_start(target, source).then_inc(weights_in, 16)
            for kind, n in vector_order:
                if kind == "piece":
                    adj_arrived(act, n)
                    if diag_pieces(n + 1) > diag_pieces(n):
                        act.wait_ge(diag_added, diag_pieces(n + 1))
                    if n % PPS == 0 and n // PPS >= NSB - 2:
                        act.wait_ge(group_done, sum(k[0] <= n // PPS - 4 for k in groups))
                    nc.scalar.activation(a8_piece(n), stage[:, n % STAGES, :], ACT.Copy, saturate=False).then_inc(piece_cast, 1)
                    if n >= 4 and on_pool(n - 4):
                        sum_difference(n - 4)
                if kind == "group" and n in firsts:
                    store_first(n)
                if kind == "count":
                    for m in range(PIECES - 4, PIECES):
                        if on_pool(m):
                            sum_difference(m)
            with act.If(is_inexact(act)):
                f_store(act)

            act.wait_ge(consts_cast, 3)
            act.dma_start(x_sorted.rearrange("(n p s) w -> p n (s w)", p=P, s=2),
                          blank[:, :, :].rearrange("p s w -> p (s w)").unsqueeze(1).to_broadcast([P, MT, 2 * W])
                          ).then_inc(rows_zeroed, 16)
            act.dma_start(out[N:N + ROWS, :].rearrange("(s p) d -> p s d", p=P), blank[:, :, 0:D]).then_inc(out_sent, 16)
            for e in range(E):
                act.wait_ge(w1_in[e % 2], 16 * (e // 2 + 1))
                if e == 0:
                    act.wait_ge(group_done, sum(g[0] <= NSB - 3 for g in groups))
                nc.scalar.activation(w1s[:, e, 0], w1_in_sb[:, e % 2, :].rearrange("p (k n) -> p k n", k=KD),
                                     ACT.Copy, scale=W_SCALE).then_inc(w1_high, 1)
            for k in range(2):
                load_x_again(k)
            for kind, k in ending():
                if kind == "groups":
                    for g in last_groups[k]:
                        if g in firsts:
                            store_first(g)
                elif kind == "z":
                    act.wait_ge(z_used, k + 1)
                    act.dma_start(out_tiles[:, ORDER[k] * TPS:(ORDER[k] + 1) * TPS, :],
                                  feats_rows[:, ORDER[k] * TPS:(ORDER[k] + 1) * TPS, :]).then_inc(out_sent, 16)
                    if k + 2 < NSB:
                        load_x_again(k + 2)
                elif kind == "t":
                    act.wait_ge(turned, k + 1)
                    if k:
                        act.wait_ge(gate_done, k)
                    for half in range(KD):
                        last = nc.scalar.activation(xT_gate[:, half, :], banks[4 + half][:, :], ACT.Copy)
                    last.then_inc(turned_out, 1)
                elif kind == "route":
                    act.wait_ge(gap_ready, k + 1)
                    nc.scalar.activation(exp_gap[:, :], top_gap[:, :], ACT.Exp).then_inc(exp_ready, 1)
            act.wait_ge(w2_in, 16 * E)
            for e in range(E):
                nc.scalar.activation(w2s[:, e, 0].rearrange("p k d -> p (k d)"), w2_in_sb[:, e * KF * D:(e + 1) * KF * D],
                                     ACT.Copy, scale=W_SCALE).then_inc(w2_high, 1)

            def xT_high_part(n, parity):
                act.wait_ge(tile_turned, n + 1)
                act.wait_ge(h_summed, n - 1 + AHEAD)
                nc.scalar.activation(xT_parts[:, parity, 0].rearrange("p k n -> p (k n)"), degree[parity][:, :],
                                     ACT.Copy).then_inc(xT_high, 1)

            def relu(n, parity, e):
                act.wait_ge(h_summed, n + 1 + AHEAD)
                act.wait_ge(h_low, n - 1 + AHEAD)
                for f in range(KF):
                    last = nc.scalar.activation(
                        h_sb[:, parity, f, :], banks[2 * parity + f // 2][:, f % 2 * ROWS:(f % 2 + 1) * ROWS], ACT.Relu,
                        bias=b1_cols[:, bass.ds(e, 1), f:f + 1].rearrange("p a b -> p (a b)"), scale=1.0 / W_SCALE)
                last.then_inc(h_relu, 1)

            def weight_rows(n, parity, slot):
                act.wait_ge(y_ready, n + 1 + AHEAD)
                for s in range(2):
                    last = nc.scalar.activation(y_sb[:, parity, s, :], y_sb[:, parity, s, :], ACT.Copy,
                                                scale=sorted_in[:, slot, s, D:D + 1])
                last.then_inc(y_weighted, 1)

            act.wait_ge(w2_low, E)
            xT_high_part(0, 0)
            xT_high_part(1, 1)
            relu(0, 0, expert_of(act, 0))
            with act.Fori(0, TURNS) as turn:
                es = experts_of(act, turn * UNROLL, UNROLL + 1, "act")
                for u in range(UNROLL):
                    n = turn * UNROLL + u
                    xT_high_part(n + 2, u % 2)
                    relu(n + 1, (u + 1) % 2, es[u + 1])
                    weight_rows(n, u % 2, u % RING)
            for n in range(TURNS * UNROLL, MT):
                if n + 2 < MT:
                    xT_high_part(n + 2, n % 2)
                if n + 1 < MT:
                    relu(n + 1, (n + 1) % 2, expert_of(act, n + 1))
                weight_rows(n, n % 2, n % RING)

        @block.vector
        def _(dve):
            links = [0]

            def link(ins):
                links[0] += 1
                ins.then_inc(chain, 1)
                dve.wait_ge(chain, links[0])

            def refine(v, y, t, u):
                link(nc.vector.tensor_tensor(t, y, y, ALU.mult))
                link(nc.vector.tensor_tensor(u, t, v, ALU.mult))
                link(nc.vector.tensor_scalar(t, u, -0.5, 1.5, ALU.mult, ALU.add))
                link(nc.vector.tensor_tensor(y, y, t, ALU.mult))

            def add_group(n):
                _, i, half, _, _ = groups[n]
                dve.wait_ge(group_done, n + 1)
                if i < NSB - 1:
                    dve.wait_ge(first_stored, KD * (i + 1))
                else:
                    dve.wait_ge(last_cleared, 1)
                if rests.index(n):
                    dve.wait_ge(rest_added, rests.index(n))
                nc.vector.tensor_tensor(feats_cols[:, i, half, :], feats_cols[:, i, half, :],
                                        banks[n % PSUM_GROUPS][:, :], ALU.add).then_inc(rest_added, 1)

            def linear_and_norm(k):
                i = ORDER[k]
                dve.wait_ge(z_done, k + 1)
                dve.wait_ge(x_again_in[k % 2], 16 * (k // 2 + 1))
                tiles = [feats_rows[:, i * TPS + j, :] for j in range(TPS)]
                for j in range(TPS):
                    last = nc.vector.scalar_tensor_tensor(
                        out=tiles[j], in0=degree[j // 2][:, j % 2 * D:(j % 2 + 1) * D],
                        scalar=dis_down[:, i * TPS + j:i * TPS + j + 1], in1=bias_rows[:, :], op0=ALU.mult, op1=ALU.add)
                link(last)
                for j in range(TPS):
                    last = nc.vector.scalar_tensor_tensor(out=tiles[j], in0=tiles[j], scalar=0.0, in1=x_again[k % 2][:, j, :],
                                                          op0=ALU.max, op1=ALU.add)
                last.then_inc(z_used, 1)
                dve.wait_ge(z_used, k + 1)
                for j in range(TPS):
                    last = nc.vector.bn_stats(stats_z[:, j, :], tiles[j])
                link(last)
                for j in range(TPS):
                    last = nc.vector.bn_aggr(mv_z[:, j, :], stats_z[:, j, :])
                link(last)
                v, t, u, y = (newton_z[:, n, 0:TPS] for n in range(4))
                nc.vector.tensor_scalar(v, mv_z[:, :, 1], EPS, None, ALU.add).then_inc(norm_safe, 1)
                dve.wait_ge(norm_safe, k + 1)
                dve.wait_ge(norm_pow, k + 1)
                refine(v, y, t, u)
                if k == 0:
                    dve.wait_ge(group_done, sum(g[0] <= NSB - 2 for g in groups))
                for j in range(TPS):
                    last = nc.vector.tensor_scalar(normed(k)[:, j, :], tiles[j], mv_z[:, j, 0:1], newton_z[:, 3, j:j + 1],
                                                   ALU.subtract, ALU.mult)
                last.then_inc(normed_ready, 1)

            def top_two(k):
                dve.wait_ge(gate_done, k + 1)
                rows = slice(k * TPS, (k + 1) * TPS)
                nc.vector.tensor_tensor(logits[:, rows, :], banks[3][:, 0:TPS * E].rearrange("p (t e) -> p t e", e=E),
                                        gate_bias[:, :].unsqueeze(1).to_broadcast([P, TPS, E]),
                                        ALU.add).then_inc(logits_read, 1)
                dve.wait_ge(logits_read, k + 1)
                for t in range(rows.start, rows.stop):
                    last = nc.vector.max(top8[:, t, :], logits[:, t, :])
                link(last)
                for t in range(rows.start, rows.stop):
                    last = nc.vector.max_index(idx8[:, t, :], top8[:, t, :], logits[:, t, :])
                link(last)

            def route():
                nc.vector.tensor_tensor(top_gap[:, :], top8[:, :, 1], top8[:, :, 0], ALU.subtract).then_inc(gap_ready, 1)
                for r in range(TOP):
                    link(nc.vector.tensor_copy(idxf[:, r, :], idx8[:, :, r]))
                    link(nc.vector.tensor_tensor(mask[:, r], iota_e.unsqueeze(1).to_broadcast([P, NT, E]),
                                                 idxf[:, r, :].unsqueeze(2).to_broadcast([P, NT, E]), ALU.is_equal))
                nc.vector.tensor_tensor(mask_sum[:, :, :], mask[:, 0], mask[:, 1], ALU.add).then_inc(masks_ready, 1)
                dve.wait_ge(exp_ready, 1)
                link(nc.vector.tensor_scalar(denom[:, :], exp_gap[:, :], 1.0, None, ALU.add))
                link(nc.vector.reciprocal(pair_w[:, 0, :], denom[:, :]))
                nc.vector.tensor_tensor(pair_w[:, 1, :], exp_gap[:, :], pair_w[:, 0, :], ALU.mult).then_inc(pair_w_ready, 1)
                nc.vector.tensor_copy(rows_out[:, :, D], pair_w[:, 0, :]).then_inc(meta_ready, 1)
                nc.vector.tensor_copy(rows_out[:, :, D + 1].bitcast(i32), con[:, C_TOKEN:C_TOKEN + NT]).then_inc(meta_ready, 1)
                dve.wait_ge(ranked, 1)
                link(nc.vector.tensor_copy(rank[:, :, :], banks[3][:, 0:NT * E].rearrange("p (t e) -> p t e", e=E)))
                nc.vector.tensor_scalar(counts_i[:, 0, :], banks[3][:, NT * E:(NT + 1) * E], float(ROWS - 1), None,
                                        ALU.add).then_inc(rank_read, 1)
                dve.wait_ge(rank_read, 1)
                link(nc.vector.tensor_scalar(counts_i[:, 1, :], counts_i[:, 0, :], ROWS.bit_length() - 1, None,
                                             ALU.logical_shift_right))
                link(nc.vector.tensor_copy(tiles_f[:, :], counts_i[:, 1, :]))
                link(nc.vector.tensor_tensor(prod8[:, :, :], before, tiles_f[:, :].unsqueeze(1).to_broadcast([P, E, E]),
                                             ALU.mult))
                link(nc.vector.tensor_reduce(base[:, :], prod8[:, :, :], AXX, ALU.add))
                link(nc.vector.scalar_tensor_tensor(out=ends[:, :], in0=base[:, :], scalar=1.0 / ROWS, in1=tiles_f[:, :],
                                                    op0=ALU.mult, op1=ALU.add))
                link(nc.vector.tensor_tensor(rank[:, :, :], rank[:, :, :],
                                             base[:, :].unsqueeze(1).to_broadcast([P, NT, E]), ALU.add))
                for r in range(TOP):
                    link(nc.vector.tensor_tensor(picked[:, :, :], mask[:, r], rank[:, :, :], ALU.mult))
                    link(nc.vector.tensor_reduce(slot_f[:, r, :], picked[:, :, :], AXX, ALU.add))
                link(nc.vector.tensor_tensor(over[:, :, :], iota_t.unsqueeze(2).to_broadcast([P, MT, E]),
                                             ends[:, :].unsqueeze(1).to_broadcast([P, MT, E]), ALU.is_ge))
                link(nc.vector.tensor_reduce(owner[:, :], over[:, :, :], AXX, ALU.add))
                link(nc.vector.tensor_scalar(tile_e[:, 0:MT], owner[:, :], float(E - 1), None, ALU.min))
                nc.vector.tensor_copy(slot_of[:, :, :], slot_f[:, :, :]).then_inc(slots_ready, 1)
                dve.wait_ge(pair_w_ready, 1)

            dve.wait_ge(x_in, 16)
            for kind, n in vector_order:
                if kind == "norm":
                    if n:
                        dve.wait_ge(xs_ready, n)
                    for k in range(TPS):
                        last = nc.vector.bn_stats(stats[:, k, :], feats_rows[:, n * TPS + k, :])
                    link(last)
                    for k in range(TPS):
                        last = nc.vector.bn_aggr(mv[:, n * TPS + k, :], stats[:, k, :])
                    link(last)
                    cols = slice(n * TPS, (n + 1) * TPS)
                    link(nc.vector.tensor_scalar(var[:, cols], mv[:, cols, 1], EPS, XS_SCALE ** -2, ALU.add, ALU.mult))
                elif kind == "piece":
                    if on_pool(n):
                        continue
                    dve.wait_ge(piece_cast, n + 1)
                    if n:
                        dve.wait_ge(piece_checked, sum(not on_pool(m) for m in range(n)))
                    nc.vector.scalar_tensor_tensor(
                        out=scratch[:, :].bitcast(mybir.dt.uint8), in0=stage[:, n % STAGES, :], scalar=1.0, in1=a8_piece(n),
                        op0=ALU.mult, op1=ALU.not_equal, accum_out=mism[:, n:n + 1]).then_inc(piece_checked, 1)
                elif kind == "prep":
                    dve.wait_ge(deg_summed, PPS * (n + 1))
                    cols = slice(n * TPS, (n + 1) * TPS)
                    v, y = newton[:, 0, :], newton[:, 3, :]
                    nc.vector.tensor_copy(deg[:, cols], degree[n % 2][:, 0:TPS]).then_inc(deg_read, 1)
                    dve.wait_ge(deg_read, n + 1)
                    nc.vector.scalar_tensor_tensor(out=v, in0=deg[:, cols], scalar=DEG_FLOOR, in1=var[:, cols],
                                                   op0=ALU.max, op1=ALU.mult).then_inc(deg_safe, 1)
                    dve.wait_ge(deg_safe, n + 1)
                    dve.wait_ge(pow_ready, n + 1)
                    refine(v, y, newton[:, 1, :], newton[:, 2, :])
                    link(nc.vector.scalar_tensor_tensor(out=rscale[:, cols], in0=deg[:, cols], scalar=0.0, in1=y,
                                                        op0=ALU.is_gt, op1=ALU.mult))
                    for j in range(n * TPS, (n + 1) * TPS):
                        last = nc.vector.tensor_scalar(feats_rows[:, j, :], feats_rows[:, j, :], mv[:, j, 0:1],
                                                       rscale[:, j:j + 1], ALU.subtract, ALU.mult)
                    link(last)
                    rows = feats_rows[:, cols, :]
                    link(nc.vector.tensor_copy(xs[:, cols, 0, :], rows))
                    nc.vector.tensor_tensor(xs[:, cols, 1, :], rows, xs[:, cols, 0, :],
                                            ALU.subtract).then_inc(xs_ready, 1)
                elif kind == "count":
                    dve.wait_ge(piece_checked, sum(not on_pool(m) for m in range(PIECES)))
                    dve.wait_ge(difference_summed, sum(on_pool(m) for m in range(PIECES)))
                    link(nc.vector.tensor_scalar(mism[:, :], mism[:, :], 0.0, None, ALU.not_equal))
                    nc.vector.tensor_reduce(found[:, :], mism[:, :], AXX, ALU.add).then_inc(found_ready, 1)
                elif kind == "flag":
                    dve.wait_ge(found_summed, 1)
                    nc.vector.tensor_copy(inexact[0:1, :], banks[5][0:1, 0:1]).then_inc(inexact_ready, 1)
                elif kind == "down" and n == 0:
                    nc.vector.tensor_scalar(newton_z[:, 0, :], deg[:, :], DEG_FLOOR, XS_SCALE ** 2, ALU.max,
                                            ALU.mult).then_inc(down_safe, 1)
                elif kind == "down":
                    dve.wait_ge(down_safe, 1)
                    dve.wait_ge(down_pow, 1)
                    refine(newton_z[:, 0, :], newton_z[:, 3, :], newton_z[:, 1, :], newton_z[:, 2, :])
                    nc.vector.scalar_tensor_tensor(out=dis_down[:, :], in0=deg[:, :], scalar=0.0, in1=newton_z[:, 3, :],
                                                   op0=ALU.is_gt, op1=ALU.mult).then_inc(down_ready, 1)
                    dve.wait_ge(down_ready, 1)
                elif kind == "group" and n in rests:
                    add_group(n)
            with dve.If(is_inexact(dve)):
                f_scale(dve)
            dve.wait_ge(weights_in, 16 * 6)
            nc.vector.tensor_copy(earlier[:, :], con[:, 0:P]).then_inc(consts_cast, 1)
            nc.vector.memset(all_ones[:, :], 1.0).then_inc(consts_cast, 1)
            dve.wait_ge(zeros_made, 1)
            nc.vector.tensor_copy(blank[:, :, D + 1].bitcast(i32), con[:, C_TOKEN + NT:C_TOKEN + NT + 2]).then_inc(consts_cast, 1)
            for e in range(E):
                dve.wait_ge(w1_high, e + 1)
                nc.vector.scalar_tensor_tensor(out=w1s[:, e, 1], in0=w1_in_sb[:, e % 2, :].rearrange("p (k n) -> p k n", k=KD),
                                               scalar=W_SCALE, in1=w1s[:, e, 0], op0=ALU.mult,
                                               op1=ALU.subtract).then_inc(w1_low, 1)
            iota_e = con[:, C_IOTA_E:C_IOTA_E + E]
            iota_t = con[:, C_IOTA_T:C_IOTA_T + MT]
            before = con[:, C_BEFORE:C_BEFORE + E * E].rearrange("p (a b) -> p a b", a=E)
            for kind, k in ending():
                if kind == "groups":
                    for g in last_groups[k]:
                        if g in rests:
                            add_group(g)
                elif kind == "z":
                    linear_and_norm(k)
                elif kind == "g":
                    top_two(k)
                elif kind == "route":
                    route()
            for e in range(E):
                dve.wait_ge(w2_high, e + 1)
                nc.vector.scalar_tensor_tensor(out=w2s[:, e, 1].rearrange("p k d -> p (k d)"),
                                               in0=w2_in_sb[:, e * KF * D:(e + 1) * KF * D], scalar=W_SCALE,
                                               in1=w2s[:, e, 0].rearrange("p k d -> p (k d)"), op0=ALU.mult,
                                               op1=ALU.subtract).then_inc(w2_low, 1)

            for k in range(NSB):
                dve.wait_ge(scattered_first[k], 16 * TPS)
                rows = slice(k * TPS, (k + 1) * TPS)
                nc.vector.tensor_copy(rows_out[:, rows, D], pair_w[:, 1, rows]).then_inc(second_weights, 1)

            def xT_low_part(n, parity):
                dve.wait_ge(xT_high, n + 1)
                nc.vector.tensor_tensor(xT_parts[:, parity, 1].rearrange("p k n -> p (k n)"), degree[parity][:, :],
                                        xT_parts[:, parity, 0].rearrange("p k n -> p (k n)"),
                                        ALU.subtract).then_inc(xT_low, 1)

            def split_hidden(n, parity):
                dve.wait_ge(h_relu, n + 1)
                dve.wait_ge(y_summed, n - 1 + AHEAD)
                nc.vector.tensor_copy(h_parts[:, parity, 0], h_sb[:, parity]).then_inc(h_high, 1)
                dve.wait_ge(h_high, n + 1)
                nc.vector.tensor_tensor(h_parts[:, parity, 1], h_sb[:, parity], h_parts[:, parity, 0],
                                        ALU.subtract).then_inc(h_low, 1)

            def expert_out(n, parity, e):
                dve.wait_ge(y_summed, n + 1 + AHEAD)
                dve.wait_ge(landed, n + LANDED)
                for s in range(2):
                    last = nc.vector.scalar_tensor_tensor(
                        out=y_sb[:, parity, s, :], in0=banks[4 + parity][:, s * D:(s + 1) * D], scalar=1.0 / W_SCALE,
                        in1=b2_rows[:, bass.ds(e, 1), :].rearrange("p a d -> p (a d)"), op0=ALU.mult, op1=ALU.add)
                last.then_inc(y_ready, 1)

            dve.wait_ge(b2_in, 16)
            dve.sem_inc(h_low, AHEAD)
            dve.sem_inc(y_ready, AHEAD)
            xT_low_part(0, 0)
            xT_low_part(1, 1)
            split_hidden(0, 0)
            with dve.Fori(0, TURNS) as turn:
                es = experts_of(dve, turn * UNROLL, UNROLL, "dve")
                for u in range(UNROLL):
                    n = turn * UNROLL + u
                    xT_low_part(n + 2, u % 2)
                    split_hidden(n + 1, (u + 1) % 2)
                    expert_out(n, u % 2, es[u])
            for n in range(TURNS * UNROLL, MT):
                if n + 2 < MT:
                    xT_low_part(n + 2, n % 2)
                if n + 1 < MT:
                    split_hidden(n + 1, (n + 1) % 2)
                expert_out(n, n % 2, expert_of(dve, n))

        @block.tensor
        def _(pe):
            def product_group(n):
                b, i, half, c0, c1 = groups[n]
                pe.wait_ge(xs_ready, b + 1)
                if n >= PSUM_GROUPS:
                    wait_evacuated(pe, n - PSUM_GROUPS)
                tiles = range(c0 * TPS, c1 * TPS)
                for j in tiles:
                    for part in range(2):
                        last = nc.tensor.matmul(
                            banks[n % PSUM_GROUPS][:, :], xs[:, j, part, half * P:(half + 1) * P],
                            a8[:, slots[i, j // TPS], j % TPS * SB:(j % TPS + 1) * SB],
                            start=(j == tiles[0] and part == 0), stop=(j == tiles[-1] and part == 1))
                last.then_inc(group_done, 1)

            pe.wait_ge(ident_made, 5)
            for kind, n in tensor_order:
                if kind == "piece":
                    pe.wait_ge(piece_cast, n + 1)
                    b, p = divmod(n, PPS)
                    if p == 0 and b >= 2:
                        pe.wait_ge(deg_read, b - 1)
                    for k in range(PIECE_TILES):
                        for i in range(TPS):
                            last = nc.tensor.matmul(
                                degree[b % 2][:, i:i + 1], a8_piece(n)[:, k * SB + i * P:k * SB + (i + 1) * P], ones8[:, :],
                                start=(p == 0 and k == 0 and i == 0), stop=(p == PPS - 1 and k == PIECE_TILES - 1),
                                skip_group_check=True)
                    last.then_inc(deg_summed, 1)
                elif kind == "count":
                    pe.wait_ge(found_ready, 1)
                    nc.tensor.matmul(banks[5][0:1, 0:1], found[:, :], ones32[:, :], start=True,
                                     stop=True).then_inc(found_summed, 1)
                else:
                    product_group(n)
            with pe.If(is_inexact(pe)):
                f_products(pe)

            pe.wait_ge(weights_in, 16 * 6)
            pe.wait_ge(consts_cast, 2)
            for kind, k in ending():
                if kind == "groups":
                    for g in last_groups[k]:
                        product_group(g)
                elif kind == "z":
                    i = ORDER[k]
                    for g in last_groups[k]:
                        wait_evacuated(pe, g)
                    if k == 0:
                        pe.wait_ge(deg_read, NSB)
                    else:
                        pe.wait_ge(z_used, k)
                    for j in range(TPS):
                        for half in range(KD):
                            last = nc.tensor.matmul(degree[j // 2][:, j % 2 * D:(j % 2 + 1) * D],
                                                    feats_cols[:, i, half, j * P:(j + 1) * P], wT[:, half, :],
                                                    start=half == 0, stop=half == KD - 1)
                    last.then_inc(z_done, 1)
                elif kind == "t":
                    pe.wait_ge(normed_ready, k + 1)
                    if k:
                        pe.wait_ge(turned_out, k)
                    for half in range(KD):
                        for j in range(TPS):
                            last = nc.tensor.transpose(banks[4 + half][:, j * P:(j + 1) * P],
                                                       normed(k)[:, j, half * P:(half + 1) * P], ident[:, :])
                    last.then_inc(turned, 1)
                elif kind == "g":
                    pe.wait_ge(turned_out, k + 1)
                    if k:
                        pe.wait_ge(logits_read, k)
                    for j in range(TPS):
                        for half in range(KD):
                            last = nc.tensor.matmul(banks[3][:, j * E:(j + 1) * E], xT_gate[:, half, j * P:(j + 1) * P],
                                                    gate[:, half, :], start=half == 0, stop=half == KD - 1)
                    last.then_inc(gate_done, 1)
                else:
                    pe.wait_ge(masks_ready, 1)
                    pe.wait_ge(logits_read, NSB)
                    flat = mask_sum[:, :, :].rearrange("p t e -> p (t e)")
                    nc.tensor.matmul(banks[3][:, 0:NT * E], earlier[:, :], flat, start=True, stop=False,
                                     skip_group_check=True)
                    for t in range(1, NT):
                        nc.tensor.matmul(banks[3][:, t * E:NT * E], all_ones[:, :], flat[:, 0:(NT - t) * E],
                                         start=False, stop=t == NT - 1, skip_group_check=True)
                    for t in range(NT):
                        last = nc.tensor.matmul(banks[3][:, NT * E:(NT + 1) * E], all_ones[:, :], mask_sum[:, t, :],
                                                start=False, stop=t == NT - 1, skip_group_check=True)
                    last.then_inc(ranked, 1)

            def turn_rows(n, slot, loads, parity):
                pe.wait_ge(sorted_load[slot], loads)
                for half in range(KD):
                    for s in range(2):
                        last = nc.tensor.transpose(degree[parity][:, half * ROWS + s * P:half * ROWS + (s + 1) * P],
                                                   sorted_in[:, slot, s, half * P:(half + 1) * P], ident[:, :])
                last.then_inc(tile_turned, 1)

            def hidden(n, parity, e):
                pe.wait_ge(xT_low, n + 1)
                for f in range(KF):
                    for half in range(KD):
                        for x_part, w_part in ((0, 0), (1, 0), (0, 1)):
                            last = nc.tensor.matmul(
                                banks[2 * parity + f // 2][:, f % 2 * ROWS:(f % 2 + 1) * ROWS],
                                w1s[:, bass.ds(e, 1), w_part, half, f * P:(f + 1) * P].rearrange("p a n -> p (a n)"),
                                xT_parts[:, parity, x_part, half, :],
                                start=(half == 0 and x_part == w_part), stop=(half == KD - 1 and w_part == 1))
                last.then_inc(h_summed, 1)

            def down(n, parity, e):
                pe.wait_ge(h_low, n + 1 + AHEAD)
                pe.wait_ge(y_ready, n - 1 + AHEAD)
                for s in range(2):
                    for f in range(KF):
                        for h_part, w_part in ((0, 0), (0, 1), (1, 0)):
                            last = nc.tensor.matmul(
                                banks[4 + parity][:, s * D:(s + 1) * D], h_parts[:, parity, h_part, f, s * P:(s + 1) * P],
                                w2s[:, bass.ds(e, 1), w_part, f, :].rearrange("p a n -> p (a n)"),
                                start=(f == 0 and h_part == w_part), stop=(f == KF - 1 and h_part == 1))
                last.then_inc(y_summed, 1)

            pe.wait_ge(w2_low, E)
            pe.wait_ge(slots_ready, 1)
            pe.sem_inc(h_summed, AHEAD)
            pe.sem_inc(y_summed, AHEAD)
            turn_rows(0, 0, 16, 0)
            turn_rows(1, 1, 16, 1)
            hidden(0, 0, expert_of(pe, 0))
            with pe.Fori(0, TURNS) as turn:
                es = experts_of(pe, turn * UNROLL, UNROLL + 1, "pe")
                for u in range(UNROLL):
                    n = turn * UNROLL + u
                    turn_rows(n + 2, (u + 2) % RING, turn * 16 + 16 * ((u + 2) // RING + 1), u % 2)
                    hidden(n + 1, (u + 1) % 2, es[u + 1])
                    down(n, u % 2, es[u])
            for n in range(TURNS * UNROLL, MT):
                if n + 2 < MT:
                    turn_rows(n + 2, (n + 2) % RING, 16 * ((n + 2) // RING + 1), n % 2)
                if n + 1 < MT:
                    hidden(n + 1, (n + 1) % 2, expert_of(pe, n + 1))
                down(n, n % 2, expert_of(pe, n))


def kernel(x, adj, L0_gnn_W, L0_gnn_b, L0_ffn_gate_w, L0_ffn_gate_b, L0_ffn_w1, L0_ffn_b1, L0_ffn_w2, L0_ffn_b2):
    import numpy as np
    import concourse.bacc as bacc
    from concourse.bass_utils import run_bass_kernel_spmd

    pieces = np.ascontiguousarray(np.asarray(adj).reshape(NSB, SB, PPS, PIECE_TILES, P).transpose(0, 2, 4, 3, 1))
    arrays = {
        "x": np.ascontiguousarray(x), "adj_pieces": pieces.reshape(PIECES, P, PIECE),
        "gnn_wT": np.ascontiguousarray(np.asarray(L0_gnn_W).T), "gnn_b": np.ascontiguousarray(L0_gnn_b).reshape(1, D),
        "gate_w": np.ascontiguousarray(L0_ffn_gate_w), "gate_b": np.ascontiguousarray(L0_ffn_gate_b).reshape(1, E),
        "w1": np.ascontiguousarray(L0_ffn_w1), "b1": np.ascontiguousarray(np.asarray(L0_ffn_b1).reshape(E, KF, P).transpose(2, 0, 1)),
        "w2": np.ascontiguousarray(L0_ffn_w2), "b2": np.ascontiguousarray(L0_ffn_b2).reshape(E * D),
    }
    con = np.zeros((P, NCONST), np.float32)
    con[:, 0:P] = np.triu(np.ones((P, P)), 1)
    con[:, C_IOTA_E:C_IOTA_E + E] = np.arange(E)
    con[:, C_IOTA_T:C_IOTA_T + MT] = np.arange(MT)
    con[:, C_BEFORE:C_BEFORE + E * E] = ROWS * np.tril(np.ones((E, E)), -1).reshape(-1)
    tiles = [i * TPS + j for i in ORDER for j in range(TPS)] + [NT, NT + 1]
    con[:, C_TOKEN:] = np.arange(P)[:, None] + P * np.array(tiles)
    arrays["consts"] = con
    nc = bacc.Bacc("TRN2", target_bir_lowering=False, num_devices=1)
    ins = [nc.dram_tensor(name, a.shape, mybir.dt.from_np(a.dtype), kind="ExternalInput").ap()
           for name, a in arrays.items()]
    out = nc.dram_tensor("out", (N + ROWS, D), mybir.dt.float32, kind="ExternalOutput").ap()
    build(nc, *ins, out)
    r = run_bass_kernel_spmd(nc, [arrays], core_ids=[0])
    return r.results[0]["out"][:N]
```

```python
from contextlib import ExitStack

import concourse.bass as bass
from concourse import mybir

N, D = 4096, 256
E, F = 8, 512
P = 128
SB = 512
NSB = N // SB
NT = N // P
TPS = SB // P
KD = D // P
KF = F // P
PIECE_TILES = 2
PIECES = NT // PIECE_TILES * NSB
PPS = PIECES // NSB
PIECE = PIECE_TILES * SB
PIECE_TIME = 1.8
FIRST_SLACK, REST_SLACK = 10.0, 3.0
STAGES = 7
F_STAGES = 4
STREAM_BANKS = 5
LAST_BANKS = 3
XS_SCALE = 128.0
W_SCALE = 64.0
EPS = 1e-5
ORDER = [NSB - 1] + list(range(NSB - 1))
PART_ENDS = (3, 6, 8)
TOP = 2
ROWS = 2 * P
MT = N * TOP // ROWS + E - 1
BLANK_AFTER = (125, 126, 127)
BLANKS = len(BLANK_AFTER)
W = D + 2
C_IOTA_E = P
C_IOTA_T = C_IOTA_E + E
C_BEFORE = C_IOTA_T + MT
C_TOKEN = C_BEFORE + E * E
NCONST = C_TOKEN + NT + 2
UNROLL = 8
TURNS = (MT - 3) // UNROLL
AHEAD = 2
RING = UNROLL
LANDED = 4
DEG_FLOOR = 2.0 ** -10


def adjacency_slots():
    kept = sorted(((b, c) for b in range(NSB - 2) for c in range(NSB)), key=lambda k: (max(k), k))
    slots = {k: n for n, k in enumerate(kept)}
    for b in (NSB - 2, NSB - 1):
        for c in range(NSB):
            slots[b, c] = (b - (NSB - 2)) * NSB + c
    return slots, len(kept)


def timeline():
    groups = []
    for b in range(NSB):
        for i in ORDER if b == NSB - 1 else [b] + list(range(b)):
            groups += [(b, i, half, 0 if i == b else b, b + 1) for half in range(KD)]
    arrive = [5.0 + PIECE_TIME * (n + 1) for n in range(PIECES)]
    tensor, timed = [], [(arrive[n], 0, ("piece", n)) for n in range(PIECES)]
    timed += [(arrive[PPS * b + 6], 0, ("norm", b)) for b in range(NSB)]
    count_time = arrive[-1] + 6.0
    timed += [(count_time, 3, ("count", 0)), (arrive[NT], 3, ("blank", 0))]
    now, piece, counted = 0.0, 0, False
    scaled = [0.0] * NSB
    for b in range(NSB):
        for g, (step, i, half, c0, c1) in enumerate(groups):
            if step != b:
                continue
            while piece < PIECES and (piece < PPS * (b + 1) or arrive[piece] <= now):
                now = max(now, arrive[piece]) + 0.3
                tensor.append(("piece", piece))
                piece += 1
                if piece % PPS == 0:
                    timed.append((now, 1, ("prep", piece // PPS - 1)))
                    scaled[piece // PPS - 1] = now + 4.5
                    if piece == PIECES:
                        timed += [(now + 1.0, 3, ("down", 0)), (now + 9.0, 3, ("down", 1))]
            if piece == PIECES and now > count_time and not counted:
                counted = True
                tensor.append(("count", 0))
                timed.append((now + 1.0, 3, ("flag", 0)))
            tensor.append(("group", g))
            now = max(now, scaled[b]) + 1.75 * (c1 - c0)
            timed.append((now + (FIRST_SLACK if step == i else REST_SLACK), 2, ("group", g)))
    last = [g for g, k in enumerate(groups) if k[0] == NSB - 1]
    tensor = [event for event in tensor if event not in [("group", g) for g in last]]
    timed = [event for _, _, event in sorted(timed) if event not in [("group", g) for g in last]]
    return groups, tensor, timed


def ending():
    order = []
    for k in range(NSB + 3):
        if k < NSB:
            order.append(("groups", k))
        for kind, lag in (("z", 1), ("route", 3), ("t", 2), ("g", 3)):
            if kind == "route" and k - lag in PART_ENDS:
                order.append((kind, PART_ENDS.index(k - lag)))
            elif kind != "route" and 0 <= k - lag < NSB:
                order.append((kind, k - lag))
    return order + [("route", len(PART_ENDS) - 1)]


def tiles_of(part):
    return range(PART_ENDS[part - 1] * TPS if part else 0, PART_ENDS[part] * TPS)


def build(nc, x, adj_pieces, gnn_wT, gnn_b, gate_w, gate_b, w1, b1, w2, b2, consts, out):
    f32, f16, f8, bf16 = mybir.dt.float32, mybir.dt.float16, mybir.dt.float8e4, mybir.dt.bfloat16
    i32, u32 = mybir.dt.int32, mybir.dt.uint32
    ALU = mybir.AluOpType
    ACT = mybir.ActivationFunctionType
    AXX = mybir.AxisListType.X
    groups, tensor_order, vector_order = timeline()
    slots, nslots = adjacency_slots()
    ng = len(groups)
    last_groups = {k: [g for g, (b, i, *_) in enumerate(groups) if b == NSB - 1 and i == ORDER[k]]
                   for k in range(NSB)}

    ctx = ExitStack()
    with ctx:
        def sb(name, shape, dt):
            return ctx.enter_context(nc.sbuf_tensor(name, shape, dt))

        def sem(name):
            return ctx.enter_context(nc.semaphore(name))

        feats = sb("feats", [P, NSB, TPS * D], f32)
        xs = sb("xs", [P, NT, 2, D], f16)
        pool_words = sb("pool_words", [P, nslots * SB + NT * W - NT * D], f32)
        a8 = pool_words[:, 0:nslots * SB].bitcast(f8).rearrange("p (s n) -> p s n", s=nslots)
        stage = sb("stage", [P, STAGES, PIECE], f32)
        scratch = sb("scratch", [P, 256], f32)
        unequal = sb("unequal", [P, 2, PIECE], mybir.dt.bfloat16)
        mism = sb("mism", [P, PIECES], f32)
        ones32 = sb("ones32", [P, 1], f32)
        found = sb("found", [P, 1], f32)
        inexact = sb("inexact", [P, 1], i32)
        ident = sb("ident", [P, P], f32)
        ones8 = sb("ones8", [P, 1], f8)
        stats = sb("stats", [P, TPS, 6], f32)
        stats_z = sb("stats_z", [P, TPS, 6], f32)
        mv_z = sb("mv_z", [P, TPS, 2], f32)
        newton_z = sb("newton_z", [P, 4, NT], f32)
        norm_scale = sb("norm_scale", [P, 2, TPS], f32)
        norm_shift = sb("norm_shift", [P, 2, TPS], f32)
        mv = sb("mv", [P, NT, 2], f32)
        newton = sb("newton", [P, 4, TPS], f32)
        minus_half = sb("minus_half", [P, NT], f32)
        var = sb("var", [P, NT], f32)
        deg = sb("deg", [P, NT], f32)
        rscale = sb("rscale", [P, NT], f32)

        dis_down = sb("dis_down", [P, NT], f32)
        wT = sb("wT", [P, KD, D], f32)
        bias_rows = sb("bias_rows", [P, D], f32)
        gate = sb("gate", [P, KD, E], f32)
        gate_bias = sb("gate_bias", [P, E], f32)
        b1_cols = sb("b1_cols", [P, E, KF], f32)
        blank = sb("blank", [P, 2, W], f32)
        con = sb("con", [P, NCONST], f32)
        earlier = sb("earlier", [P, P], bf16)
        all_ones = sb("all_ones", [P, P], bf16)
        mask_sum = sb("mask_sum", [P, NT, E], bf16)
        idxf = sb("idxf", [P, TOP, NT], f32)
        counts_i = sb("counts_i", [P, 2, E], i32)
        total = sb("total", [P, E], f32)
        room = sb("room", [P, E], f32)
        offset = sb("offset", [P, E], f32)
        rows_used = sb("rows_used", [P, 1], f32)
        ended = sb("ended", [P, MT], f32)
        ended_i = sb("ended_i", [P, MT], i32)
        shift = sb("shift", [P, E], f32)
        grown = sb("grown", [P, E], f32)
        tiles_f = sb("tiles_f", [P, E], f32)
        prod8 = sb("prod8", [P, E, E], f32)
        base = sb("base", [P, E], f32)
        ends = sb("ends", [P, E], f32)
        over = scratch[:, :].bitcast(bf16)[:, 0:MT * E].rearrange("p (t e) -> p t e", e=E)
        owner = sb("owner", [P, MT], f32)
        slot_f = sb("slot_f", [P, TOP, NT], f32)
        top_gap = sb("top_gap", [P, NT], f32)
        exp_gap = sb("exp_gap", [P, NT], f32)
        denom = sb("denom", [P, NT], f32)
        slot_of = sb("slot_of", [P, TOP, NT], u32)
        pair_w = sb("pair_w", [P, TOP, NT], f32)
        tile_e = sb("tile_e", [P, -(-MT // 8) * 8], i32)

        def words(first_slot, slots_):
            return pool_words[:, first_slot * SB:(first_slot + slots_) * SB]

        w2s = words(0, 16).bitcast(f16).rearrange("p (e s k n) -> p e s k n", e=E, s=2, k=KF)
        w1s = words(16, 16).bitcast(f16).rearrange("p (e s k n) -> p e s k n", e=E, s=2, k=KD)
        rows_out = pool_words[:, 32 * SB:32 * SB + NT * W].rearrange("p (t w) -> p t w", w=W)
        xs_words = xs[:, :, :, :].rearrange("p t s d -> p (t s d)").bitcast(f32)
        w2_in_sb = xs_words
        logits = stage[:, 0, 0:NT * E].rearrange("p (t e) -> p t e", e=E)
        top8 = stage[:, 0, NT * E:2 * NT * E].rearrange("p (t e) -> p t e", e=E)
        idx8 = stage[:, 0, 2 * NT * E:3 * NT * E].bitcast(u32).rearrange("p (t e) -> p t e", e=E)
        rank = stage[:, 0, 3 * NT * E:4 * NT * E].rearrange("p (t e) -> p t e", e=E)
        mask = stage[:, 1, 0:TOP * NT * E].rearrange("p (r t e) -> p r t e", r=TOP, e=E)
        picked = stage[:, 1, TOP * NT * E:(TOP + 1) * NT * E].rearrange("p (t e) -> p t e", e=E)
        x_again = [stage[:, 2 + n, :].rearrange("p (t d) -> p t d", d=D) for n in range(2)]
        def w1_in_sb(e):
            return stage[:, (0, 1, 4, 5)[e % len(w1_in)], :]

        xT_gate = stage[:, 6, :].rearrange("p (k n) -> p k n", k=KD)
        feats_words = feats[:, :, :].rearrange("p b n -> p (b n)")
        b2_rows = feats_words[:, 0:E * D].rearrange("p (e d) -> p e d", e=E)
        y_sb = feats_words[:, E * D:E * D + 4 * D].rearrange("p (r s d) -> p r s d", r=2, s=2)
        sorted_in = feats_words[:, E * D + 4 * D:E * D + 4 * D + RING * 2 * W].rearrange("p (r s w) -> p r s w", r=RING, s=2)
        h_start = 2 * KD * ROWS
        h_parts_start = h_start + 2 * KF * ROWS
        xT_parts = xs_words[:, 0:h_start].bitcast(f16).rearrange("p (r s k n) -> p r s k n", r=2, s=2, k=KD)
        h_sb = xs_words[:, h_start:h_parts_start].rearrange("p (r k n) -> p r k n", r=2, k=KF)
        h_parts = xs_words[:, h_parts_start:h_parts_start + 2 * KF * ROWS].bitcast(f16).rearrange(
            "p (r s k n) -> p r s k n", r=2, s=2, k=KF)

        def normed(k):
            return rows_out[:, k * TPS:(k + 1) * TPS, 0:D]

        x_sorted = nc.dram_tensor("x_sorted", (MT * ROWS, W), f32).ap()

        degree = [ctx.enter_context(nc.psum_tensor(f"degree{n}", [P, 512], f32)) for n in range(2)]
        banks = [ctx.enter_context(nc.psum_tensor(f"bank{n}", [P, 512], f32)) for n in range(6)]

        x_in = sem("x_in")

        adj_in = [sem(f"adj_in{n}") for n in range(STAGES)]
        last_cleared = sem("last_cleared")
        found_ready = sem("found_ready")
        found_summed = sem("found_summed")
        inexact_ready = sem("inexact_ready")
        down_safe = sem("down_safe")
        down_pow = sem("down_pow")
        down_ready = sem("down_ready")
        f_x_in = sem("f_x_in")
        f_adj_in = [sem(f"f_adj_in{n}") for n in range(F_STAGES)]
        f_piece_used = sem("f_piece_used")
        f_deg_read = sem("f_deg_read")
        f_pow_safe = sem("f_pow_safe")
        f_pow_ready = sem("f_pow_ready")
        f_rows_ready = sem("f_rows_ready")
        f_stored = sem("f_stored")
        f_cleared = sem("f_cleared")
        f_turned = sem("f_turned")
        f_added = sem("f_added")
        f_chain = sem("f_chain")
        chain = sem("chain")
        ident_made = sem("ident_made")
        deg_read = sem("deg_read")
        pow_ready = sem("pow_ready")
        diag_added = sem("diag_added")
        piece_cast = sem("piece_cast")
        piece_checked = sem("piece_checked")
        piece_compared = sem("piece_compared")
        difference_summed = sem("difference_summed")
        deg_summed = sem("deg_summed")
        deg_safe = sem("deg_safe")
        xs_ready = sem("xs_ready")
        group_done = sem("group_done")
        first_stored = sem("first_stored")
        rest_added = sem("rest_added")
        weights_in = sem("weights_in")
        zeros_made = sem("zeros_made")
        blank_made = sem("blank_made")
        rows_zeroed = sem("rows_zeroed")
        x_again_in = [sem(f"x_again_in{n}") for n in range(2)]
        w1_in = [sem(f"w1_in{n}") for n in range(4)]
        w1_high = sem("w1_high")
        w1_low = sem("w1_low")
        w2_in = sem("w2_in")
        w2_high = sem("w2_high")
        w2_low = sem("w2_low")
        b2_in = sem("b2_in")
        norm_safe = sem("norm_safe")
        deviation = sem("deviation")
        z_done = sem("z_done")
        z_used = sem("z_used")
        scale_ready = sem("scale_ready")
        normed_ready = sem("normed_ready")
        turned = sem("turned")
        turned_out = sem("turned_out")
        gate_done = sem("gate_done")
        logits_read = sem("logits_read")
        masks_ready = sem("masks_ready")
        ranked = sem("ranked")
        rank_read = sem("rank_read")
        slots_ready = sem("slots_ready")
        tiles_known = sem("tiles_known")
        gap_ready = sem("gap_ready")
        exp_ready = sem("exp_ready")
        pair_w_ready = sem("pair_w_ready")
        consts_cast = sem("consts_cast")
        scattered_first = [sem(f"scattered_first{n}") for n in range(NSB)]
        meta_ready = sem("meta_ready")
        second_weights = sem("second_weights")
        scattered = sem("scattered")
        sorted_load = [sem(f"sorted_load{n}") for n in range(RING)]
        tile_turned = sem("tile_turned")
        xT_high = sem("xT_high")
        xT_low = sem("xT_low")
        h_summed = sem("h_summed")
        h_relu = sem("h_relu")
        h_high = sem("h_high")
        h_low = sem("h_low")
        y_summed = sem("y_summed")
        y_ready = sem("y_ready")
        y_weighted = sem("y_weighted")
        landed = sem("landed")
        added = sem("added")
        out_sent = sem("out_sent")

        block = ctx.enter_context(nc.Block())
        x_tiles = x.rearrange("(t p) d -> p t d", p=P)
        out_tiles = out[0:N, :].rearrange("(t p) d -> p t d", p=P)
        feats_rows = feats[:, :, :].rearrange("p b (t d) -> p (b t) d", d=D)
        feats_cols = feats[:, :, :].rearrange("p b (h i) -> p b h i", h=KD)

        firsts = [g for g in range(ng) if groups[g][0] == groups[g][1] < NSB - 1]
        rests = [g for g in range(ng) if g not in firsts]
        streamed = [g for g in range(ng) if groups[g][0] < NSB - 1]

        def bank_of(g):
            return g % STREAM_BANKS if g < len(streamed) else (g - len(streamed)) % LAST_BANKS

        def wait_evacuated(eng, g):
            if g in firsts:
                eng.wait_ge(first_stored, firsts.index(g) + 1)
            else:
                eng.wait_ge(rest_added, rests.index(g) + 1)

        def on_pool(n):
            return n % 3 == 1

        def wait_checked(eng, n):
            mine = sum(on_pool(m) == on_pool(n) for m in range(n + 1))
            eng.wait_ge(piece_compared if on_pool(n) else piece_checked, mine)

        def a8_piece(n):
            b, q = divmod(n, PPS)
            c, half = divmod(q, TPS // PIECE_TILES)
            return a8[:, slots[b, c], half * PIECE:(half + 1) * PIECE]

        def expert_of(eng, tile):
            return eng.value_load(tile_e[0:1, bass.ds(tile, 1)], min_val=0, max_val=E - 1)

        def experts_of(eng, tile, count, name):
            registers = [eng.alloc_register(f"expert_{name}_{n}") for n in range(count)]
            eng.load(registers, tile_e[0:1, bass.ds(tile, count)])
            return [eng.snap(r, min_val=0, max_val=E - 1) for r in registers]

        def adj_arrived(eng, n):
            eng.wait_ge(adj_in[n % STAGES], 16 * (n // STAGES + 1))

        def diag_pieces(n):
            return sum(m // PPS == m % PPS * PIECE_TILES // TPS for m in range(n))

        f_rows = words(0, 16).rearrange("p (t d) -> p t d", d=D)

        def is_inexact(eng):
            eng.wait_ge(inexact_ready, 1)
            return eng.value_load(inexact[0:1, 0:1], min_val=0, max_val=P * PIECES) > 0

        def wait_steps_done(eng):
            eng.wait_ge(group_done, len(streamed))
            eng.wait_ge(first_stored, len(firsts))
            eng.wait_ge(rest_added, sum(g in streamed for g in rests))
            eng.wait_ge(xs_ready, NSB)
            eng.wait_ge(last_cleared, 1)
            eng.wait_ge(down_ready, 1)
            eng.wait_ge(deg_summed, PIECES)

        def f_load(sp):
            wait_steps_done(sp)
            sp.dma_start(f_rows, x_tiles).then_inc(f_x_in, 16)
            for sweep in range(2):
                with sp.Fori(0, NSB) as b:
                    for q in range(PPS):
                        sp.wait_ge(f_piece_used, b * PPS + (sweep * PIECES + q + 1))
                        sp.dma_start(stage[:, q % F_STAGES, :],
                                     adj_pieces[bass.ds(b * PPS + q, 1)].rearrange("a p n -> (a p) n")
                                     ).then_inc(f_adj_in[q % F_STAGES], 16)
            sp.wait_ge(f_cleared, 2)

        def f_power(pool):
            for n in range(2):
                pool.wait_ge(f_pow_safe, n + 1)
                nc.gpsimd.tensor_tensor(newton_z[:, 3, :], newton_z[:, 0, :], minus_half[:, :],
                                        ALU.pow).then_inc(f_pow_ready, 1)
            pool.wait_ge(f_cleared, 2)

        def f_store(act):
            with act.Fori(0, NSB) as b:
                act.wait_ge(f_piece_used, b * PPS + (F_STAGES + PIECES + PPS))
                for half in range(KD):
                    last = nc.scalar.activation(
                        feats[:, bass.ds(b, 1), half * SB:(half + 1) * SB].rearrange("p a n -> p (a n)"),
                        banks[half][:, :], ACT.Copy)
                last.then_inc(f_stored, 1)
            act.wait_ge(f_cleared, 2)

        def f_scale(dve):
            links = [0]

            def link(ins):
                links[0] += 1
                ins.then_inc(f_chain, 1)
                dve.wait_ge(f_chain, links[0])

            def refine(v, y, t, u):
                link(nc.vector.tensor_tensor(t, y, y, ALU.mult))
                link(nc.vector.tensor_tensor(u, t, v, ALU.mult))
                link(nc.vector.tensor_scalar(t, u, -0.5, 1.5, ALU.mult, ALU.add))
                link(nc.vector.tensor_tensor(y, y, t, ALU.mult))

            wait_steps_done(dve)
            with dve.Fori(0, NSB) as b:
                dve.wait_ge(f_piece_used, b * PPS + (F_STAGES + PPS))
                nc.vector.tensor_scalar(deg[:, bass.ds(b * TPS, TPS)], degree[0][:, 0:TPS], 1.0, None,
                                        ALU.add).then_inc(f_deg_read, 1)
            dve.wait_ge(f_deg_read, NSB + 1)
            v, t, u, y = (newton_z[:, n, :] for n in range(4))
            nc.vector.tensor_scalar(v, deg[:, :], 1e-37, 1e38, ALU.max, ALU.min).then_inc(f_pow_safe, 1)
            dve.wait_ge(f_pow_safe, 1)
            dve.wait_ge(f_pow_ready, 1)
            refine(v, y, t, u)
            link(nc.vector.scalar_tensor_tensor(out=dis_down[:, :], in0=deg[:, :], scalar=0.0, in1=y,
                                                op0=ALU.is_gt, op1=ALU.mult))
            nc.vector.tensor_scalar(v, mv[:, :, 1], EPS, None, ALU.add).then_inc(f_pow_safe, 1)
            dve.wait_ge(f_pow_safe, 2)
            dve.wait_ge(f_pow_ready, 2)
            refine(v, y, t, u)
            link(nc.vector.tensor_tensor(rscale[:, :], y, dis_down[:, :], ALU.mult))
            dve.wait_ge(f_x_in, 16)
            for j in range(NT):
                last = nc.vector.tensor_scalar(f_rows[:, j, :], f_rows[:, j, :], mv[:, j, 0:1], rscale[:, j:j + 1],
                                               ALU.subtract, ALU.mult)
            last.then_inc(f_rows_ready, 1)
            dve.wait_ge(f_stored, NSB + 1)
            for b in range(NSB):
                dve.wait_ge(f_turned, b + 1)
                for half in range(KD):
                    last = nc.vector.tensor_tensor(feats_cols[:, b, half, :], feats_cols[:, b, half, :],
                                                   banks[2 + half][:, :], ALU.add)
                last.then_inc(f_added, 1)
            dve.wait_ge(f_added, NSB)
            nc.vector.memset(xs[:, :, :, :].rearrange("p t s d -> p (t s d)").bitcast(f32), 0.0).then_inc(f_cleared, 1)
            nc.vector.memset(pool_words[:, 0:nslots * SB], 0.0).then_inc(f_cleared, 1)
            dve.wait_ge(f_cleared, 2)

        def f_products(pe):
            def piece(sweep, b, q):
                pe.wait_ge(f_adj_in[q % F_STAGES], b * (16 * PPS // F_STAGES) +
                           16 * (sweep * PIECES // F_STAGES + q // F_STAGES + 1))
                return stage[:, q % F_STAGES, :].rearrange("p (k n) -> p k n", k=PIECE_TILES)

            wait_steps_done(pe)
            pe.sem_inc(f_piece_used, F_STAGES)
            pe.sem_inc(f_deg_read, 1)
            pe.sem_inc(f_stored, 1)
            with pe.Fori(0, NSB) as b:
                pe.wait_ge(f_deg_read, b + 1)
                for q in range(PPS):
                    a = piece(0, b, q)
                    for k in range(PIECE_TILES):
                        for i in range(TPS):
                            last = nc.tensor.matmul(degree[0][:, i:i + 1], a[:, k, i * P:(i + 1) * P], ones32[:, :],
                                                    start=(q == 0 and k == 0 and i == 0),
                                                    stop=(q == PPS - 1 and k == PIECE_TILES - 1), skip_group_check=True)
                    last.then_inc(f_piece_used, 1)
            pe.wait_ge(f_rows_ready, 1)
            with pe.Fori(0, NSB) as b:
                pe.wait_ge(f_stored, b + 1)
                for q in range(PPS):
                    a = piece(1, b, q)
                    for k in range(PIECE_TILES):
                        for half in range(KD):
                            last = nc.tensor.matmul(banks[half][:, :], f_rows[:, q * PIECE_TILES + k, half * P:(half + 1) * P],
                                                    a[:, k, :], start=(q == 0 and k == 0), stop=(q == PPS - 1 and k == PIECE_TILES - 1))
                    last.then_inc(f_piece_used, 1)
            for b in range(NSB):
                if b:
                    pe.wait_ge(f_added, b)
                for half in range(KD):
                    for i in range(TPS):
                        last = nc.tensor.transpose(banks[2 + half][:, i * P:(i + 1) * P],
                                                   f_rows[:, b * TPS + i, half * P:(half + 1) * P], ident[:, :])
                last.then_inc(f_turned, 1)
            pe.wait_ge(f_cleared, 2)

        @block.sync
        def _(sp):
            for n in range(PIECES):
                if n >= STAGES:
                    wait_checked(sp, n - STAGES)
                    sp.wait_ge(piece_cast, n - STAGES + 1)
                sp.dma_start(stage[:, n % STAGES, :], adj_pieces[n]).then_inc(adj_in[n % STAGES], 16)
            with sp.If(is_inexact(sp)):
                f_load(sp)
            for e in range(E):
                if e >= len(w1_in):
                    sp.wait_ge(w1_low, e - len(w1_in) + 1)
                sp.dma_start(w1_in_sb(e).rearrange("p (k f) -> p k f", k=KD),
                             w1[e].rearrange("(k p) f -> p k f", p=P)).then_inc(w1_in[e % len(w1_in)], 16)
            sp.wait_ge(group_done, ng)
            for e in range(E):
                sp.dma_start(w2_in_sb.rearrange("p (e k d) -> p e k d", e=E, k=KF)[:, e],
                             w2[e].rearrange("(k p) d -> p k d", p=P)).then_inc(w2_in, 16)
            sp.wait_ge(out_sent, 16 * (NSB + 1))
            sp.wait_ge(normed_ready, NSB)
            sp.dma_start(b2_rows.rearrange("p e d -> p (e d)"), b2.partition_broadcast(P)).then_inc(b2_in, 16)

            for k in range(NSB):
                sp.wait_ge(scattered_first[k], 16 * TPS)
            sp.wait_ge(scattered, 16 * NT)
            sp.sem_inc(landed, LANDED)

            def load_rows(tile, slot):
                sp.dma_start(sorted_in[:, slot], x_sorted[bass.ds(tile * ROWS, ROWS), :].rearrange("(p s) w -> p s w", s=2)
                             ).then_inc(sorted_load[slot], 16)

            for tile in range(3):
                load_rows(tile, tile)
            with sp.Fori(0, TURNS) as turn:
                for u in range(UNROLL):
                    sp.wait_ge(landed, turn * UNROLL + (u + 1))
                    load_rows(turn * UNROLL + (u + 3), (u + 3) % RING)
            for tile in range(TURNS * UNROLL, MT - 3):
                sp.wait_ge(landed, tile + 1)
                load_rows(tile + 3, (tile + 3) % RING)

        @block.gpsimd
        def _(pool):
            nc.gpsimd.memset(blank[:, :, :], 0.0).then_inc(zeros_made, 1)
            nc.gpsimd.memset(minus_half[:, :], -0.5).then_inc(ident_made, 1)
            nc.gpsimd.memset(ident[:, :], 0.0).then_inc(ident_made, 1)
            nc.gpsimd.memset(ones8[:, :], 1.0).then_inc(ident_made, 1)
            nc.gpsimd.memset(ones32[:, :], 1.0).then_inc(ident_made, 1)
            pool.wait_ge(ident_made, 4)
            nc.gpsimd.affine_select(out=ident[:, :], in_=ident[:, :], compare_op=ALU.not_equal, fill=1.0,
                                    base=0, pattern=[[-1, P]], channel_multiplier=1).then_inc(ident_made, 1)
            pool.wait_ge(ident_made, 5)
            for kind, n in vector_order:
                if kind == "piece" and diag_pieces(n + 1) > diag_pieces(n):
                    adj_arrived(pool, n)
                    first = n % PPS * PIECE_TILES % TPS * P
                    for t in range(PIECE_TILES):
                        part = stage[:, n % STAGES, t * SB + first + t * P:t * SB + first + (t + 1) * P]
                        last = nc.gpsimd.tensor_tensor(part, part, ident[:, :], ALU.add)
                    last.then_inc(diag_added, 1)
                if kind == "piece" and on_pool(n):
                    pool.wait_ge(piece_cast, n + 1)
                    done = sum(on_pool(m) for m in range(n))
                    if done >= 2:
                        pool.wait_ge(difference_summed, done - 1)
                    nc.gpsimd.tensor_tensor(unequal[:, done % 2, :], stage[:, n % STAGES, :], a8_piece(n),
                                            ALU.subtract).then_inc(piece_compared, 1)
                if kind == "prep":
                    pool.wait_ge(deg_safe, n + 1)
                    nc.gpsimd.tensor_tensor(newton[:, 3, 0:TPS], newton[:, 0, 0:TPS], minus_half[:, 0:TPS],
                                            ALU.pow).then_inc(pow_ready, 1)
                if kind == "down" and n == 0:
                    pool.wait_ge(down_safe, 1)
                    nc.gpsimd.tensor_tensor(newton_z[:, 3, :], newton_z[:, 0, :], minus_half[:, :],
                                            ALU.pow).then_inc(down_pow, 1)
                    pool.wait_ge(xs_ready, NSB)
                    nc.gpsimd.memset(feats[:, NSB - 1, :], 0.0).then_inc(last_cleared, 1)
            with pool.If(is_inexact(pool)):
                f_power(pool)



            def scatter(part, r, tiles):
                if r == 0 and tiles[0] == tiles_of(part)[0]:
                    pool.wait_ge(rows_zeroed, 16 * BLANKS)
                    pool.wait_ge(slots_ready, part + 1)
                    pool.wait_ge(meta_ready, 2 * part + 2)
                for t in tiles:
                    if r and t % TPS == 0:
                        pool.wait_ge(scattered_first[t // TPS], 16 * TPS)
                        nc.gpsimd.tensor_copy(rows_out[:, t:t + TPS, D], pair_w[:, 1, t:t + TPS]).then_inc(second_weights, 1)
                        pool.wait_ge(second_weights, t // TPS + 1)
                    nc.gpsimd.indirect_dma_start(
                        out=x_sorted[:, :], out_offset=bass.IndirectOffsetOnAxis(ap=slot_of[:, r, t:t + 1], axis=0),
                        in_=rows_out[:, t, :], in_offset=None).then_inc(scattered if r else scattered_first[t // TPS], 16)

            for part in range(len(PART_ENDS)):
                for r in range(TOP):
                    scatter(part, r, tiles_of(part))

            def add_rows(parity, slot):
                for s in range(2):
                    nc.gpsimd.indirect_dma_start(
                        out=out[:, :],
                        out_offset=bass.IndirectOffsetOnAxis(ap=sorted_in[:, slot, s, D + 1:D + 2].bitcast(u32), axis=0),
                        in_=y_sb[:, parity, s, :], in_offset=None, compute_op=ALU.add).then_inc(added, 16)

            pool.wait_ge(out_sent, 16 * (NSB + 1))
            pool.wait_ge(y_weighted, 1)
            pool.sem_inc(landed, 1)
            add_rows(0, 0)
            with pool.Fori(0, TURNS) as turn:
                for u in range(UNROLL):
                    pool.wait_ge(y_weighted, turn * UNROLL + (u + 2))
                    pool.wait_ge(added, turn * (32 * UNROLL) + 32 * (u + 1))
                    pool.sem_inc(landed, 1)
                    add_rows((u + 1) % 2, (u + 1) % RING)
            for tile in range(TURNS * UNROLL + 1, MT):
                pool.wait_ge(y_weighted, tile + 1)
                pool.wait_ge(added, 32 * tile)
                pool.sem_inc(landed, 1)
                add_rows(tile % 2, tile % RING)
            pool.wait_ge(added, 32 * MT)

        @block.scalar
        def _(act):
            def sum_difference(n):
                done = sum(on_pool(k) for k in range(n))
                act.wait_ge(piece_compared, done + 1)
                part = unequal[:, done % 2, :]
                nc.scalar.activation(part, part, ACT.Abs, accum_out=mism[:, n:n + 1]).then_inc(difference_summed, 1)

            def load_x_again(k):
                act.dma_start(x_again[k % 2], x_tiles[:, ORDER[k] * TPS:(ORDER[k] + 1) * TPS, :]).then_inc(x_again_in[k % 2], 16)

            def store_first(g):
                _, i, half, _, _ = groups[g]
                act.wait_ge(group_done, g + 1)
                nc.scalar.activation(feats_cols[:, i, half, :], banks[bank_of(g)][:, :],
                                     ACT.Copy).then_inc(first_stored, 1)

            act.dma_start(feats_rows, x_tiles).then_inc(x_in, 16)
            for target, source in ((wT[:, :, :], gnn_wT.rearrange("(k p) n -> p k n", p=P)),
                                   (bias_rows[:, :], gnn_b[0, :].partition_broadcast(P)),
                                   (gate[:, :, :], gate_w.rearrange("(k p) e -> p k e", p=P)),
                                   (gate_bias[:, :], gate_b[0, :].partition_broadcast(P)),
                                   (b1_cols[:, :, :], b1), (con[:, :], consts)):
                act.dma_start(target, source).then_inc(weights_in, 16)
            for kind, n in vector_order:
                if kind == "piece":
                    adj_arrived(act, n)
                    if diag_pieces(n + 1) > diag_pieces(n):
                        act.wait_ge(diag_added, diag_pieces(n + 1))
                    if n % PPS == 0 and n // PPS >= NSB - 2:
                        act.wait_ge(group_done, sum(k[0] <= n // PPS - 4 for k in groups))
                    nc.scalar.activation(a8_piece(n), stage[:, n % STAGES, :], ACT.Copy, saturate=False).then_inc(piece_cast, 1)
                    if n >= 4 and on_pool(n - 4):
                        sum_difference(n - 4)
                if kind == "group" and n in firsts:
                    store_first(n)
                if kind == "piece" and n in BLANK_AFTER:
                    act.wait_ge(blank_made, 1)
                    k = BLANK_AFTER.index(n)
                    act.dma_start(x_sorted.rearrange("(c n p s) w -> c p n (s w)", c=BLANKS, p=P, s=2)[k],
                                  blank[:, :, :].rearrange("p s w -> p (s w)").unsqueeze(1).to_broadcast(
                                      [P, MT // BLANKS, 2 * W])).then_inc(rows_zeroed, 16)
                    if k == 0:
                        act.dma_start(out[N:N + ROWS, :].rearrange("(s p) d -> p s d", p=P),
                                      blank[:, :, 0:D]).then_inc(out_sent, 16)
                if kind == "count":
                    for m in range(PIECES - 4, PIECES):
                        if on_pool(m):
                            sum_difference(m)
            with act.If(is_inexact(act)):
                f_store(act)





            for e in range(E):
                act.wait_ge(w1_in[e % len(w1_in)], 16 * (e // len(w1_in) + 1))
                if e == 0:
                    act.wait_ge(group_done, sum(g[0] <= NSB - 3 for g in groups))
                nc.scalar.activation(w1s[:, e, 0], w1_in_sb(e).rearrange("p (k n) -> p k n", k=KD),
                                     ACT.Copy, scale=W_SCALE).then_inc(w1_high, 1)
            for k in range(2):
                load_x_again(k)
            for kind, k in ending():
                if kind == "groups":
                    for g in last_groups[k]:
                        if g in firsts:
                            store_first(g)
                elif kind == "z":
                    act.wait_ge(z_used, k + 1)
                    act.dma_start(out_tiles[:, ORDER[k] * TPS:(ORDER[k] + 1) * TPS, :],
                                  feats_rows[:, ORDER[k] * TPS:(ORDER[k] + 1) * TPS, :]).then_inc(out_sent, 16)
                    if k + 2 < NSB:
                        load_x_again(k + 2)
                    act.wait_ge(norm_safe, k + 1)
                    nc.scalar.activation(newton_z[:, 3, 0:TPS], newton_z[:, 0, 0:TPS], ACT.Sqrt).then_inc(deviation, 1)
                    act.wait_ge(scale_ready, k + 1)
                    if k == 0:
                        act.wait_ge(group_done, len(streamed))
                    for j in range(TPS):
                        last = nc.scalar.activation(normed(k)[:, j, :], feats_rows[:, ORDER[k] * TPS + j, :], ACT.Identity,
                                                    bias=norm_shift[:, k % 2, j:j + 1], scale=norm_scale[:, k % 2, j:j + 1])
                    last.then_inc(normed_ready, 1)

                elif kind == "t":
                    act.wait_ge(turned, k + 1)
                    if k:
                        act.wait_ge(gate_done, k)
                    for half in range(KD):
                        last = nc.scalar.activation(xT_gate[:, half, :], banks[4 + half][:, :], ACT.Copy)
                    last.then_inc(turned_out, 1)
                elif kind == "route":
                    cols = slice(tiles_of(k).start, tiles_of(k).stop)
                    act.wait_ge(gap_ready, k + 1)
                    nc.scalar.activation(exp_gap[:, cols], top_gap[:, cols], ACT.Exp).then_inc(exp_ready, 1)
            act.wait_ge(w2_in, 16 * E)
            for e in range(E):
                nc.scalar.activation(w2s[:, e, 0].rearrange("p k d -> p (k d)"), w2_in_sb[:, e * KF * D:(e + 1) * KF * D],
                                     ACT.Copy, scale=W_SCALE).then_inc(w2_high, 1)

            def xT_high_part(n, parity):
                act.wait_ge(tile_turned, n + 1)
                act.wait_ge(h_summed, n - 1 + AHEAD)
                nc.scalar.activation(xT_parts[:, parity, 0].rearrange("p k n -> p (k n)"), degree[parity][:, :],
                                     ACT.Copy).then_inc(xT_high, 1)

            def relu(n, parity, e):
                act.wait_ge(h_summed, n + 1 + AHEAD)
                act.wait_ge(h_low, n - 1 + AHEAD)
                for f in range(KF):
                    last = nc.scalar.activation(
                        h_sb[:, parity, f, :], banks[2 * parity + f // 2][:, f % 2 * ROWS:(f % 2 + 1) * ROWS], ACT.Relu,
                        bias=b1_cols[:, bass.ds(e, 1), f:f + 1].rearrange("p a b -> p (a b)"), scale=1.0 / W_SCALE)
                last.then_inc(h_relu, 1)

            def weight_rows(n, parity, slot):
                act.wait_ge(y_ready, n + 1 + AHEAD)
                for s in range(2):
                    last = nc.scalar.activation(y_sb[:, parity, s, :], y_sb[:, parity, s, :], ACT.Copy,
                                                scale=sorted_in[:, slot, s, D:D + 1])
                last.then_inc(y_weighted, 1)

            act.wait_ge(w2_low, E)
            xT_high_part(0, 0)
            xT_high_part(1, 1)
            relu(0, 0, expert_of(act, 0))
            with act.Fori(0, TURNS) as turn:
                es = experts_of(act, turn * UNROLL, UNROLL + 1, "act")
                for u in range(UNROLL):
                    n = turn * UNROLL + u
                    xT_high_part(n + 2, u % 2)
                    relu(n + 1, (u + 1) % 2, es[u + 1])
                    weight_rows(n, u % 2, u % RING)
            for n in range(TURNS * UNROLL, MT):
                if n + 2 < MT:
                    xT_high_part(n + 2, n % 2)
                if n + 1 < MT:
                    relu(n + 1, (n + 1) % 2, expert_of(act, n + 1))
                weight_rows(n, n % 2, n % RING)

        @block.vector
        def _(dve):
            links = [0]

            def link(ins):
                links[0] += 1
                ins.then_inc(chain, 1)
                dve.wait_ge(chain, links[0])

            def refine(v, y, t, u, into=None):
                link(nc.vector.tensor_tensor(t, y, y, ALU.mult))
                link(nc.vector.tensor_tensor(u, t, v, ALU.mult))
                link(nc.vector.tensor_scalar(t, u, -0.5, 1.5, ALU.mult, ALU.add))
                link(nc.vector.tensor_tensor(y if into is None else into, y, t, ALU.mult))

            def add_group(n):
                _, i, half, _, _ = groups[n]
                dve.wait_ge(group_done, n + 1)
                if i < NSB - 1:
                    dve.wait_ge(first_stored, KD * (i + 1))
                else:
                    dve.wait_ge(last_cleared, 1)
                if rests.index(n):
                    dve.wait_ge(rest_added, rests.index(n))
                nc.vector.tensor_tensor(feats_cols[:, i, half, :], feats_cols[:, i, half, :],
                                        banks[bank_of(n)][:, :], ALU.add).then_inc(rest_added, 1)

            def linear_and_norm(k):
                i = ORDER[k]
                dve.wait_ge(z_done, k + 1)
                dve.wait_ge(x_again_in[k % 2], 16 * (k // 2 + 1))
                tiles = [feats_rows[:, i * TPS + j, :] for j in range(TPS)]
                for j in range(TPS):
                    last = nc.vector.scalar_tensor_tensor(
                        out=tiles[j], in0=degree[j // 2][:, j % 2 * D:(j % 2 + 1) * D],
                        scalar=dis_down[:, i * TPS + j:i * TPS + j + 1], in1=bias_rows[:, :], op0=ALU.mult, op1=ALU.add)
                link(last)
                for j in range(TPS):
                    last = nc.vector.scalar_tensor_tensor(out=tiles[j], in0=tiles[j], scalar=0.0, in1=x_again[k % 2][:, j, :],
                                                          op0=ALU.max, op1=ALU.add)
                last.then_inc(z_used, 1)
                dve.wait_ge(z_used, k + 1)
                for j in range(TPS):
                    last = nc.vector.bn_stats(stats_z[:, j, :], tiles[j])
                link(last)
                for j in range(TPS):
                    last = nc.vector.bn_aggr(mv_z[:, j, :], stats_z[:, j, :])
                link(last)
                v, t, u, y = (newton_z[:, n, 0:TPS] for n in range(4))
                nc.vector.tensor_scalar(v, mv_z[:, :, 1], EPS, None, ALU.add).then_inc(norm_safe, 1)
                dve.wait_ge(norm_safe, k + 1)
                dve.wait_ge(deviation, k + 1)
                link(nc.vector.reciprocal(y, y))
                if k >= 2:
                    dve.wait_ge(normed_ready, k - 1)
                scale, shift_back = norm_scale[:, k % 2, :], norm_shift[:, k % 2, :]
                refine(v, y, t, u, into=scale)
                nc.vector.scalar_tensor_tensor(out=shift_back, in0=mv_z[:, :, 0], scalar=-1.0, in1=scale, op0=ALU.mult,
                                               op1=ALU.mult).then_inc(scale_ready, 1)
                dve.wait_ge(scale_ready, k + 1)

            def top_two(k):
                dve.wait_ge(gate_done, k + 1)
                rows = slice(k * TPS, (k + 1) * TPS)
                nc.vector.tensor_tensor(logits[:, rows, :], banks[3][:, 0:TPS * E].rearrange("p (t e) -> p t e", e=E),
                                        gate_bias[:, :].unsqueeze(1).to_broadcast([P, TPS, E]),
                                        ALU.add).then_inc(logits_read, 1)
                dve.wait_ge(logits_read, k + 1)
                for t in range(rows.start, rows.stop):
                    last = nc.vector.max(top8[:, t, :], logits[:, t, :])
                link(last)
                for t in range(rows.start, rows.stop):
                    last = nc.vector.max_index(idx8[:, t, :], top8[:, t, :], logits[:, t, :])
                link(last)

            def route(part):
                tiles = tiles_of(part)
                count = len(tiles)
                cols = slice(tiles.start, tiles.stop)

                def spread(a):
                    return a.unsqueeze(1).to_broadcast([P, count, E])

                nc.vector.tensor_tensor(top_gap[:, cols], top8[:, cols, 1], top8[:, cols, 0],
                                        ALU.subtract).then_inc(gap_ready, 1)
                link(nc.vector.tensor_copy(idxf[:, :, cols], idx8[:, cols, 0:TOP].rearrange("p t r -> p r t")))
                for r in range(TOP):
                    last = nc.vector.tensor_tensor(mask[:, r, cols], spread(iota_e),
                                                   idxf[:, r, cols].unsqueeze(2).to_broadcast([P, count, E]), ALU.is_equal)
                link(last)
                nc.vector.tensor_tensor(mask_sum[:, cols, :], mask[:, 0, cols], mask[:, 1, cols], ALU.add).then_inc(masks_ready, 1)
                dve.wait_ge(exp_ready, part + 1)
                link(nc.vector.tensor_scalar(denom[:, cols], exp_gap[:, cols], 1.0, None, ALU.add))
                link(nc.vector.reciprocal(pair_w[:, 0, cols], denom[:, cols]))
                nc.vector.tensor_tensor(pair_w[:, 1, cols], exp_gap[:, cols], pair_w[:, 0, cols], ALU.mult).then_inc(pair_w_ready, 1)
                nc.vector.tensor_copy(rows_out[:, cols, D], pair_w[:, 0, cols]).then_inc(meta_ready, 1)
                nc.vector.tensor_copy(rows_out[:, cols, D + 1].bitcast(i32),
                                      con[:, C_TOKEN + cols.start:C_TOKEN + cols.stop]).then_inc(meta_ready, 1)
                dve.wait_ge(ranked, part + 1)
                nc.vector.tensor_tensor(rank[:, 0:count], banks[3][:, 0:count * E].rearrange("p (t e) -> p t e", e=E),
                                        spread(total[:, :]), ALU.add).then_inc(rank_read, 1)
                dve.wait_ge(rank_read, 2 * part + 1)
                nc.vector.tensor_tensor(total[:, :], banks[3][:, count * E:(count + 1) * E], total[:, :],
                                        ALU.add).then_inc(rank_read, 1)
                dve.wait_ge(rank_read, 2 * part + 2)
                link(nc.vector.scalar_tensor_tensor(out=counts_i[:, 0, :], in0=total[:, :], scalar=float(ROWS - 1),
                                                    in1=room[:, :], op0=ALU.add, op1=ALU.subtract))
                link(nc.vector.tensor_scalar(counts_i[:, 1, :], counts_i[:, 0, :], ROWS.bit_length() - 1, None,
                                             ALU.logical_shift_right))
                link(nc.vector.tensor_copy(tiles_f[:, :], counts_i[:, 1, :]))
                link(nc.vector.tensor_tensor(prod8[:, :, :], before, tiles_f[:, :].unsqueeze(1).to_broadcast([P, E, E]),
                                             ALU.mult))
                link(nc.vector.tensor_reduce(base[:, :], prod8[:, :, :], AXX, ALU.add))
                link(nc.vector.tensor_scalar(base[:, :], base[:, :], rows_used[:, :], None, ALU.add))
                link(nc.vector.scalar_tensor_tensor(out=ends[:, :], in0=base[:, :], scalar=1.0 / ROWS, in1=tiles_f[:, :],
                                                    op0=ALU.mult, op1=ALU.add))
                link(nc.vector.tensor_tensor(shift[:, :], base[:, :], room[:, :], ALU.subtract))
                link(nc.vector.tensor_tensor(shift[:, :], shift[:, :], offset[:, :], ALU.subtract))
                link(nc.vector.tensor_tensor(picked[:, 0:count], rank[:, 0:count], spread(room[:, :]), ALU.is_ge))
                link(nc.vector.tensor_tensor(picked[:, 0:count], picked[:, 0:count], spread(shift[:, :]), ALU.mult))
                link(nc.vector.tensor_tensor(rank[:, 0:count], rank[:, 0:count], spread(offset[:, :]), ALU.add))
                link(nc.vector.tensor_tensor(rank[:, 0:count], rank[:, 0:count], picked[:, 0:count], ALU.add))
                for r in range(TOP):
                    link(nc.vector.tensor_tensor(picked[:, 0:count], mask[:, r, cols], rank[:, 0:count], ALU.mult))
                    link(nc.vector.tensor_reduce(slot_f[:, r, cols], picked[:, 0:count], AXX, ALU.add))
                nc.vector.tensor_copy(slot_of[:, :, cols], slot_f[:, :, cols]).then_inc(slots_ready, 1)
                link(nc.vector.tensor_tensor(over[:, :, :], iota_t.unsqueeze(2).to_broadcast([P, MT, E]),
                                             ends[:, :].unsqueeze(1).to_broadcast([P, MT, E]), ALU.is_ge))
                link(nc.vector.tensor_reduce(owner[:, :], over[:, :, :], AXX, ALU.add))
                link(nc.vector.tensor_tensor(ended[:, :], ended[:, :], owner[:, :], ALU.add))
                if part == len(PART_ENDS) - 1:
                    link(nc.vector.tensor_copy(ended_i[:, :], ended[:, :]))
                    nc.vector.tensor_scalar(tile_e[:, 0:MT], ended_i[:, :], E - 1, None, ALU.bitwise_and).then_inc(tiles_known, 1)
                    dve.wait_ge(tiles_known, 1)
                else:
                    link(nc.vector.tensor_scalar(grown[:, :], tiles_f[:, :], 0.0, None, ALU.is_gt))
                    link(nc.vector.tensor_tensor(grown[:, :], grown[:, :], shift[:, :], ALU.mult))
                    link(nc.vector.tensor_tensor(offset[:, :], offset[:, :], grown[:, :], ALU.add))
                    link(nc.vector.scalar_tensor_tensor(out=room[:, :], in0=tiles_f[:, :], scalar=float(ROWS), in1=room[:, :],
                                                        op0=ALU.mult, op1=ALU.add))
                    link(nc.vector.tensor_scalar(rows_used[:, :], ends[:, E - 1:E], float(ROWS), None, ALU.mult))

            dve.wait_ge(x_in, 16)
            for kind, n in vector_order:
                if kind == "norm":
                    if n:
                        dve.wait_ge(xs_ready, n)
                    for k in range(TPS):
                        last = nc.vector.bn_stats(stats[:, k, :], feats_rows[:, n * TPS + k, :])
                    link(last)
                    for k in range(TPS):
                        last = nc.vector.bn_aggr(mv[:, n * TPS + k, :], stats[:, k, :])
                    link(last)
                    cols = slice(n * TPS, (n + 1) * TPS)
                    link(nc.vector.tensor_scalar(var[:, cols], mv[:, cols, 1], EPS, XS_SCALE ** -2, ALU.add, ALU.mult))
                elif kind == "piece":
                    if on_pool(n):
                        continue
                    dve.wait_ge(piece_cast, n + 1)
                    if n:
                        dve.wait_ge(piece_checked, sum(not on_pool(m) for m in range(n)))
                    nc.vector.scalar_tensor_tensor(
                        out=scratch[:, :].bitcast(mybir.dt.uint8), in0=stage[:, n % STAGES, :], scalar=1.0, in1=a8_piece(n),
                        op0=ALU.mult, op1=ALU.not_equal, accum_out=mism[:, n:n + 1]).then_inc(piece_checked, 1)
                elif kind == "prep":
                    dve.wait_ge(deg_summed, PPS * (n + 1))
                    cols = slice(n * TPS, (n + 1) * TPS)
                    v, y = newton[:, 0, :], newton[:, 3, :]
                    nc.vector.tensor_copy(deg[:, cols], degree[n % 2][:, 0:TPS]).then_inc(deg_read, 1)
                    dve.wait_ge(deg_read, n + 1)
                    nc.vector.scalar_tensor_tensor(out=v, in0=deg[:, cols], scalar=DEG_FLOOR, in1=var[:, cols],
                                                   op0=ALU.max, op1=ALU.mult).then_inc(deg_safe, 1)
                    dve.wait_ge(deg_safe, n + 1)
                    dve.wait_ge(pow_ready, n + 1)
                    refine(v, y, newton[:, 1, :], newton[:, 2, :])
                    link(nc.vector.scalar_tensor_tensor(out=rscale[:, cols], in0=deg[:, cols], scalar=0.0, in1=y,
                                                        op0=ALU.is_gt, op1=ALU.mult))
                    for j in range(n * TPS, (n + 1) * TPS):
                        last = nc.vector.tensor_scalar(feats_rows[:, j, :], feats_rows[:, j, :], mv[:, j, 0:1],
                                                       rscale[:, j:j + 1], ALU.subtract, ALU.mult)
                    link(last)
                    rows = feats_rows[:, cols, :]
                    link(nc.vector.tensor_copy(xs[:, cols, 0, :], rows))
                    nc.vector.tensor_tensor(xs[:, cols, 1, :], rows, xs[:, cols, 0, :],
                                            ALU.subtract).then_inc(xs_ready, 1)
                elif kind == "blank":
                    dve.wait_ge(zeros_made, 1)
                    dve.wait_ge(weights_in, 16 * 6)
                    nc.vector.tensor_copy(blank[:, :, D + 1].bitcast(i32),
                                          con[:, C_TOKEN + NT:C_TOKEN + NT + 2]).then_inc(blank_made, 1)
                elif kind == "count":
                    dve.wait_ge(piece_checked, sum(not on_pool(m) for m in range(PIECES)))
                    dve.wait_ge(difference_summed, sum(on_pool(m) for m in range(PIECES)))
                    link(nc.vector.tensor_scalar(mism[:, :], mism[:, :], 0.0, None, ALU.not_equal))
                    nc.vector.tensor_reduce(found[:, :], mism[:, :], AXX, ALU.add).then_inc(found_ready, 1)
                elif kind == "flag":
                    dve.wait_ge(found_summed, 1)
                    nc.vector.tensor_copy(inexact[0:1, :], banks[5][0:1, 0:1]).then_inc(inexact_ready, 1)
                elif kind == "down" and n == 0:
                    nc.vector.tensor_scalar(newton_z[:, 0, :], deg[:, :], DEG_FLOOR, XS_SCALE ** 2, ALU.max,
                                            ALU.mult).then_inc(down_safe, 1)
                elif kind == "down":
                    dve.wait_ge(down_safe, 1)
                    dve.wait_ge(down_pow, 1)
                    refine(newton_z[:, 0, :], newton_z[:, 3, :], newton_z[:, 1, :], newton_z[:, 2, :])
                    nc.vector.scalar_tensor_tensor(out=dis_down[:, :], in0=deg[:, :], scalar=0.0, in1=newton_z[:, 3, :],
                                                   op0=ALU.is_gt, op1=ALU.mult).then_inc(down_ready, 1)
                    dve.wait_ge(down_ready, 1)
                elif kind == "group" and n in rests:
                    add_group(n)
            with dve.If(is_inexact(dve)):
                f_scale(dve)
            dve.wait_ge(weights_in, 16 * 6)
            nc.vector.tensor_copy(earlier[:, :], con[:, 0:P]).then_inc(consts_cast, 1)
            nc.vector.memset(all_ones[:, :], 1.0).then_inc(consts_cast, 1)

            for e in range(E):
                dve.wait_ge(w1_high, e + 1)
                nc.vector.scalar_tensor_tensor(out=w1s[:, e, 1], in0=w1_in_sb(e).rearrange("p (k n) -> p k n", k=KD),
                                               scalar=W_SCALE, in1=w1s[:, e, 0], op0=ALU.mult,
                                               op1=ALU.subtract).then_inc(w1_low, 1)
            link(nc.vector.memset(total[:, :], 0.0))
            link(nc.vector.memset(room[:, :], 0.0))
            link(nc.vector.memset(offset[:, :], 0.0))
            link(nc.vector.memset(rows_used[:, :], 0.0))
            link(nc.vector.memset(ended[:, :], 0.0))
            iota_e = con[:, C_IOTA_E:C_IOTA_E + E]
            iota_t = con[:, C_IOTA_T:C_IOTA_T + MT]
            before = con[:, C_BEFORE:C_BEFORE + E * E].rearrange("p (a b) -> p a b", a=E)
            for kind, k in ending():
                if kind == "groups":
                    for g in last_groups[k]:
                        if g in rests:
                            add_group(g)
                elif kind == "z":
                    linear_and_norm(k)
                elif kind == "g":
                    top_two(k)
                elif kind == "route":
                    route(k)
            for e in range(E):
                dve.wait_ge(w2_high, e + 1)
                nc.vector.scalar_tensor_tensor(out=w2s[:, e, 1].rearrange("p k d -> p (k d)"),
                                               in0=w2_in_sb[:, e * KF * D:(e + 1) * KF * D], scalar=W_SCALE,
                                               in1=w2s[:, e, 0].rearrange("p k d -> p (k d)"), op0=ALU.mult,
                                               op1=ALU.subtract).then_inc(w2_low, 1)

            def xT_low_part(n, parity):
                dve.wait_ge(xT_high, n + 1)
                nc.vector.tensor_tensor(xT_parts[:, parity, 1].rearrange("p k n -> p (k n)"), degree[parity][:, :],
                                        xT_parts[:, parity, 0].rearrange("p k n -> p (k n)"),
                                        ALU.subtract).then_inc(xT_low, 1)

            def split_hidden(n, parity):
                dve.wait_ge(h_relu, n + 1)
                dve.wait_ge(y_summed, n - 1 + AHEAD)
                nc.vector.tensor_copy(h_parts[:, parity, 0], h_sb[:, parity]).then_inc(h_high, 1)
                dve.wait_ge(h_high, n + 1)
                nc.vector.tensor_tensor(h_parts[:, parity, 1], h_sb[:, parity], h_parts[:, parity, 0],
                                        ALU.subtract).then_inc(h_low, 1)

            def expert_out(n, parity, e):
                dve.wait_ge(y_summed, n + 1 + AHEAD)
                dve.wait_ge(landed, n + LANDED)
                for s in range(2):
                    last = nc.vector.scalar_tensor_tensor(
                        out=y_sb[:, parity, s, :], in0=banks[4 + parity][:, s * D:(s + 1) * D], scalar=1.0 / W_SCALE,
                        in1=b2_rows[:, bass.ds(e, 1), :].rearrange("p a d -> p (a d)"), op0=ALU.mult, op1=ALU.add)
                last.then_inc(y_ready, 1)

            dve.wait_ge(b2_in, 16)
            dve.sem_inc(h_low, AHEAD)
            dve.sem_inc(y_ready, AHEAD)
            xT_low_part(0, 0)
            xT_low_part(1, 1)
            split_hidden(0, 0)
            with dve.Fori(0, TURNS) as turn:
                es = experts_of(dve, turn * UNROLL, UNROLL, "dve")
                for u in range(UNROLL):
                    n = turn * UNROLL + u
                    xT_low_part(n + 2, u % 2)
                    split_hidden(n + 1, (u + 1) % 2)
                    expert_out(n, u % 2, es[u])
            for n in range(TURNS * UNROLL, MT):
                if n + 2 < MT:
                    xT_low_part(n + 2, n % 2)
                if n + 1 < MT:
                    split_hidden(n + 1, (n + 1) % 2)
                expert_out(n, n % 2, expert_of(dve, n))

        @block.tensor
        def _(pe):
            def product_group(n):
                b, i, half, c0, c1 = groups[n]
                pe.wait_ge(xs_ready, b + 1)
                earlier_groups = [g for g in range(n) if bank_of(g) == bank_of(n)]
                if earlier_groups:
                    wait_evacuated(pe, earlier_groups[-1])
                tiles = range(c0 * TPS, c1 * TPS)
                for j in tiles:
                    for part in range(2):
                        last = nc.tensor.matmul(
                            banks[bank_of(n)][:, :], xs[:, j, part, half * P:(half + 1) * P],
                            a8[:, slots[i, j // TPS], j % TPS * SB:(j % TPS + 1) * SB],
                            start=(j == tiles[0] and part == 0), stop=(j == tiles[-1] and part == 1))
                last.then_inc(group_done, 1)

            pe.wait_ge(ident_made, 5)
            for kind, n in tensor_order:
                if kind == "piece":
                    pe.wait_ge(piece_cast, n + 1)
                    b, p = divmod(n, PPS)
                    if p == 0 and b >= 2:
                        pe.wait_ge(deg_read, b - 1)
                    for k in range(PIECE_TILES):
                        for i in range(TPS):
                            last = nc.tensor.matmul(
                                degree[b % 2][:, i:i + 1], a8_piece(n)[:, k * SB + i * P:k * SB + (i + 1) * P], ones8[:, :],
                                start=(p == 0 and k == 0 and i == 0), stop=(p == PPS - 1 and k == PIECE_TILES - 1),
                                skip_group_check=True)
                    last.then_inc(deg_summed, 1)
                elif kind == "count":
                    pe.wait_ge(found_ready, 1)
                    nc.tensor.matmul(banks[5][0:1, 0:1], found[:, :], ones32[:, :], start=True,
                                     stop=True).then_inc(found_summed, 1)
                else:
                    product_group(n)
            with pe.If(is_inexact(pe)):
                f_products(pe)

            pe.wait_ge(weights_in, 16 * 6)
            pe.wait_ge(consts_cast, 2)
            pe.wait_ge(first_stored, len(firsts))
            for kind, k in ending():
                if kind == "groups":
                    for g in last_groups[k]:
                        product_group(g)
                elif kind == "z":
                    i = ORDER[k]
                    for g in last_groups[k]:
                        wait_evacuated(pe, g)
                    if k == 0:
                        pe.wait_ge(deg_read, NSB)
                    else:
                        pe.wait_ge(z_used, k)
                    for j in range(TPS):
                        for half in range(KD):
                            last = nc.tensor.matmul(degree[j // 2][:, j % 2 * D:(j % 2 + 1) * D],
                                                    feats_cols[:, i, half, j * P:(j + 1) * P], wT[:, half, :],
                                                    start=half == 0, stop=half == KD - 1)
                    last.then_inc(z_done, 1)
                elif kind == "t":
                    pe.wait_ge(normed_ready, k + 1)
                    if k:
                        pe.wait_ge(turned_out, k)
                    for half in range(KD):
                        for j in range(TPS):
                            last = nc.tensor.transpose(banks[4 + half][:, j * P:(j + 1) * P],
                                                       normed(k)[:, j, half * P:(half + 1) * P], ident[:, :])
                    last.then_inc(turned, 1)
                elif kind == "g":
                    pe.wait_ge(turned_out, k + 1)
                    if k:
                        pe.wait_ge(logits_read, k)
                    if k in PART_ENDS:
                        pe.wait_ge(rank_read, 2 * PART_ENDS.index(k) + 2)
                    for j in range(TPS):
                        for half in range(KD):
                            last = nc.tensor.matmul(banks[3][:, j * E:(j + 1) * E], xT_gate[:, half, j * P:(j + 1) * P],
                                                    gate[:, half, :], start=half == 0, stop=half == KD - 1)
                    last.then_inc(gate_done, 1)
                else:
                    tiles = tiles_of(k)
                    count = len(tiles)
                    pe.wait_ge(masks_ready, k + 1)
                    pe.wait_ge(logits_read, PART_ENDS[k])
                    flat = mask_sum[:, tiles.start:tiles.stop, :].rearrange("p t e -> p (t e)")
                    nc.tensor.matmul(banks[3][:, 0:count * E], earlier[:, :], flat, start=True, stop=False,
                                     skip_group_check=True)
                    for t in range(1, count):
                        nc.tensor.matmul(banks[3][:, t * E:count * E], all_ones[:, :], flat[:, 0:(count - t) * E],
                                         start=False, stop=t == count - 1, skip_group_check=True)
                    for t in tiles:
                        last = nc.tensor.matmul(banks[3][:, count * E:(count + 1) * E], all_ones[:, :], mask_sum[:, t, :],
                                                start=False, stop=t == tiles[-1], skip_group_check=True)
                    last.then_inc(ranked, 1)

            def turn_rows(n, slot, loads, parity):
                pe.wait_ge(sorted_load[slot], loads)
                for half in range(KD):
                    for s in range(2):
                        last = nc.tensor.transpose(degree[parity][:, half * ROWS + s * P:half * ROWS + (s + 1) * P],
                                                   sorted_in[:, slot, s, half * P:(half + 1) * P], ident[:, :])
                last.then_inc(tile_turned, 1)

            def hidden(n, parity, e):
                pe.wait_ge(xT_low, n + 1)
                for f in range(KF):
                    for half in range(KD):
                        for x_part, w_part in ((0, 0), (1, 0), (0, 1)):
                            last = nc.tensor.matmul(
                                banks[2 * parity + f // 2][:, f % 2 * ROWS:(f % 2 + 1) * ROWS],
                                w1s[:, bass.ds(e, 1), w_part, half, f * P:(f + 1) * P].rearrange("p a n -> p (a n)"),
                                xT_parts[:, parity, x_part, half, :],
                                start=(half == 0 and x_part == w_part), stop=(half == KD - 1 and w_part == 1))
                last.then_inc(h_summed, 1)

            def down(n, parity, e):
                pe.wait_ge(h_low, n + 1 + AHEAD)
                pe.wait_ge(y_ready, n - 1 + AHEAD)
                for s in range(2):
                    for f in range(KF):
                        for h_part, w_part in ((0, 0), (0, 1), (1, 0)):
                            last = nc.tensor.matmul(
                                banks[4 + parity][:, s * D:(s + 1) * D], h_parts[:, parity, h_part, f, s * P:(s + 1) * P],
                                w2s[:, bass.ds(e, 1), w_part, f, :].rearrange("p a n -> p (a n)"),
                                start=(f == 0 and h_part == w_part), stop=(f == KF - 1 and h_part == 1))
                last.then_inc(y_summed, 1)

            pe.wait_ge(w2_low, E)
            pe.wait_ge(tiles_known, 1)
            pe.sem_inc(h_summed, AHEAD)
            pe.sem_inc(y_summed, AHEAD)
            turn_rows(0, 0, 16, 0)
            turn_rows(1, 1, 16, 1)
            hidden(0, 0, expert_of(pe, 0))
            with pe.Fori(0, TURNS) as turn:
                es = experts_of(pe, turn * UNROLL, UNROLL + 1, "pe")
                for u in range(UNROLL):
                    n = turn * UNROLL + u
                    turn_rows(n + 2, (u + 2) % RING, turn * 16 + 16 * ((u + 2) // RING + 1), u % 2)
                    hidden(n + 1, (u + 1) % 2, es[u + 1])
                    down(n, u % 2, es[u])
            for n in range(TURNS * UNROLL, MT):
                if n + 2 < MT:
                    turn_rows(n + 2, (n + 2) % RING, 16 * ((n + 2) // RING + 1), n % 2)
                if n + 1 < MT:
                    hidden(n + 1, (n + 1) % 2, expert_of(pe, n + 1))
                down(n, n % 2, expert_of(pe, n))


def kernel(x, adj, L0_gnn_W, L0_gnn_b, L0_ffn_gate_w, L0_ffn_gate_b, L0_ffn_w1, L0_ffn_b1, L0_ffn_w2, L0_ffn_b2):
    import numpy as np
    import concourse.bacc as bacc
    from concourse.bass_utils import run_bass_kernel_spmd

    pieces = np.ascontiguousarray(np.asarray(adj).reshape(NSB, SB, PPS, PIECE_TILES, P).transpose(0, 2, 4, 3, 1))
    arrays = {
        "x": np.ascontiguousarray(x), "adj_pieces": pieces.reshape(PIECES, P, PIECE),
        "gnn_wT": np.ascontiguousarray(np.asarray(L0_gnn_W).T), "gnn_b": np.ascontiguousarray(L0_gnn_b).reshape(1, D),
        "gate_w": np.ascontiguousarray(L0_ffn_gate_w), "gate_b": np.ascontiguousarray(L0_ffn_gate_b).reshape(1, E),
        "w1": np.ascontiguousarray(L0_ffn_w1), "b1": np.ascontiguousarray(np.asarray(L0_ffn_b1).reshape(E, KF, P).transpose(2, 0, 1)),
        "w2": np.ascontiguousarray(L0_ffn_w2), "b2": np.ascontiguousarray(L0_ffn_b2).reshape(E * D),
    }
    con = np.zeros((P, NCONST), np.float32)
    con[:, 0:P] = np.triu(np.ones((P, P)), 1)
    con[:, C_IOTA_E:C_IOTA_E + E] = np.arange(E)
    con[:, C_IOTA_T:C_IOTA_T + MT] = np.arange(MT)
    con[:, C_BEFORE:C_BEFORE + E * E] = ROWS * np.tril(np.ones((E, E)), -1).reshape(-1)
    tiles = [i * TPS + j for i in ORDER for j in range(TPS)] + [NT, NT + 1]
    con[:, C_TOKEN:] = np.arange(P)[:, None] + P * np.array(tiles)
    arrays["consts"] = con
    nc = bacc.Bacc("TRN2", target_bir_lowering=False, num_devices=1)
    ins = [nc.dram_tensor(name, a.shape, mybir.dt.from_np(a.dtype), kind="ExternalInput").ap()
           for name, a in arrays.items()]
    out = nc.dram_tensor("out", (N + ROWS, D), mybir.dt.float32, kind="ExternalOutput").ap()
    build(nc, *ins, out)
    r = run_bass_kernel_spmd(nc, [arrays], core_ids=[0])
    return r.results[0]["out"][:N]
```
